# Optimizing a Trainium2 kernel written in Bass

```python
import numpy as np
import jax
import jax.numpy as jnp

def _softmax(x, axis=-1):
    return jax.nn.softmax(x, axis=axis)

def _gelu(x):
    return jax.nn.gelu(x, approximate=True)

def _silu(x):
    return jax.nn.silu(x)

def _sigmoid(x):
    return jax.nn.sigmoid(x)

def _layernorm(x, axis=-1, eps=1e-05):
    m = jnp.mean(x, axis=axis, keepdims=True)
    v = jnp.var(x, axis=axis, keepdims=True)
    return (x - m) / jnp.sqrt(v + eps)

def _scatter_add(tgt, idx, src, axis=0):
    return tgt.at[idx].add(src)

def _segment_sum(src, seg, n):
    return jax.ops.segment_sum(src, seg, n)
kernel_name = 'mk_decoder_preln_d4_seqx_r8_7e2dc1'

def setup_inputs(seed: int=0):
    np.random.seed(seed)
    _w = jnp.asarray

    def _rec_inputs():
        import jax
        import jax.numpy as jnp
        _rk = jax.random.key(seed)
        x = -0.0002928 + 1 * jax.random.normal(jax.random.fold_in(_rk, 1), (4, 256, 128), jnp.float32)
        _lenS = 256 - jax.random.randint(jax.random.fold_in(_rk, 7), (4,), 0, max(1, 256 // 4) + 1, jnp.int32)
        _lenS2 = 256 - jax.random.randint(jax.random.fold_in(_rk, 8), (4,), 0, max(1, 256 // 4) + 1, jnp.int32)
        _ctx_1024P = jax.random.normal(jax.random.fold_in(_rk, 11), (4, 16, 128), jnp.float32)
        _ctx_1024c = jax.random.dirichlet(jax.random.fold_in(_rk, 511), 0.3 * jnp.ones((16,), jnp.float32), (4, 256))
        _ctx_1024t = jnp.einsum('bsk,bkd->bsd', _ctx_1024c, _ctx_1024P)
        _ctx_1024t = _ctx_1024t * jax.lax.rsqrt(jnp.mean(jnp.square(_ctx_1024t)) + 1e-12) * 0.953939
        ctx_1024 = -1.39393e-06 + 0.999914 * (_ctx_1024t + 0.3 * jax.random.normal(jax.random.fold_in(_rk, 611), (4, 256, 128), jnp.float32))
        itok_BxS_0_511 = jax.random.randint(jax.random.fold_in(_rk, 12), (4, 256), 0, 64, jnp.int32)
        return (x, ctx_1024, itok_BxS_0_511)
    x, ctx_1024, itok_BxS_0_511 = _rec_inputs()

    def _L0_attn_setup():
        import math
        import jax, jax.numpy as jnp
        import numpy as np
        B, L, DIM, HEADS = (4, 256, 128, 8)
        HEAD = DIM // HEADS
        SCALE_BASE = 512.0
        EPS = 1e-05

        def _xpos(x, downscale=False):
            l, dh = (x.shape[-2], x.shape[-1])
            half = dh // 2
            pos = jnp.arange(l, dtype=x.dtype)
            base = (jnp.arange(0, dh, 2, dtype=x.dtype) + 0.4 * dh) / (1.4 * dh)
            scale = base[None, :] ** (pos[:, None] / SCALE_BASE)
            inv_freq = 1.0 / 10000.0 ** (jnp.arange(half, dtype=x.dtype) / half)
            sinusoid = pos[:, None] * inv_freq[None, :]
            sin, cos = (jnp.sin(sinusoid), jnp.cos(sinusoid))
            if downscale:
                scale = 1.0 / scale
            s = jnp.repeat(sin * scale, 2, axis=-1)
            c = jnp.repeat(cos * scale, 2, axis=-1)
            x1, x2 = (x[..., ::2], x[..., 1::2])
            rot = jnp.stack([-x2, x1], axis=-1).reshape(x.shape)
            return x * c + rot * s

        def _decay_mask(l, gammas):
            n = jnp.arange(l)[:, None]
            m = jnp.arange(l)[None, :]
            lg = jnp.log(gammas)
            expo = (n - m).astype(jnp.float32)[None, :, :] * lg[:, None, None]
            return jnp.where((n >= m)[None], jnp.exp(expo), 0.0)
        key = jax.random.key(seed)
        ks = jax.random.split(key, 6)
        d = DIM
        return {'X': jax.random.normal(ks[0], (B, L, DIM), dtype=jnp.float32), 'W_Q': jax.random.normal(ks[1], (HEADS, DIM, HEAD), dtype=jnp.float32) / d, 'W_K': jax.random.normal(ks[2], (HEADS, DIM, HEAD), dtype=jnp.float32) / d, 'W_V': jax.random.normal(ks[3], (HEADS, DIM, HEAD), dtype=jnp.float32) / d, 'W_G': jax.random.normal(ks[4], (DIM, DIM), dtype=jnp.float32) / d, 'W_O': jax.random.normal(ks[5], (DIM, DIM), dtype=jnp.float32) / d, 'gn_weight': jnp.ones((DIM,), dtype=jnp.float32), 'gn_bias': jnp.zeros((DIM,), dtype=jnp.float32)}
    _L0_attn_all = _L0_attn_setup()
    _L0_attn_in = {k: v for k, v in _L0_attn_all.items() if k in ('W_Q', 'W_K', 'W_V', 'W_G', 'W_O', 'gn_weight', 'gn_bias')}
    del _L0_attn_all

    def _L0_xattn_setup():
        import jax, jax.numpy as jnp
        import numpy as np
        D_MODEL = 128
        N_HEAD = 16
        D_HEAD = D_MODEL // N_HEAD
        key = jax.random.key(seed)
        ks = jax.random.split(key, 6)
        B, L, M = (2, 256, 256)
        q = jax.random.normal(ks[0], (B, L, D_MODEL), dtype=jnp.float32)
        kv = jax.random.normal(ks[1], (B, L, D_MODEL), dtype=jnp.float32)
        mem = jax.random.normal(ks[2], (B, M, D_MODEL), dtype=jnp.float32)
        s = 1.0 / np.sqrt(D_MODEL)
        w_q = jax.random.normal(ks[3], (D_MODEL, D_MODEL), dtype=jnp.float32) * s
        w_kv = jax.random.normal(ks[4], (D_MODEL, 2 * D_HEAD), dtype=jnp.float32) * s
        w_concat = jax.random.normal(ks[5], (D_MODEL, D_MODEL), dtype=jnp.float32) * s
        return {'q': q, 'kv': kv, 'mem': mem, 'w_q': w_q, 'w_kv': w_kv, 'w_concat': w_concat}
    _L0_xattn_all = _L0_xattn_setup()
    _L0_xattn_in = {k: v for k, v in _L0_xattn_all.items() if k in ('w_q', 'w_kv', 'w_concat')}
    del _L0_xattn_all

    def _L0_ffn_setup():
        import jax, jax.numpy as jnp
        import numpy as np
        B, S, H = (2, 256, 128)
        N, F, SF, K = (16, 128, 512, 1)
        key = jax.random.key(seed)
        ks = jax.random.split(key, 7)
        std = 0.02
        return {'hidden_states': jax.random.normal(ks[0], (B, S, H), dtype=jnp.float32), 'router_w': jax.random.normal(ks[1], (N, H), dtype=jnp.float32) * std, 'gate_up_proj': jax.random.normal(ks[2], (N, H, 2 * F), dtype=jnp.float32) * std, 'down_proj': jax.random.normal(ks[3], (N, F, H), dtype=jnp.float32) * std, 'shared_gate_w': jax.random.normal(ks[4], (SF, H), dtype=jnp.float32) * std, 'shared_up_w': jax.random.normal(ks[5], (SF, H), dtype=jnp.float32) * std, 'shared_down_w': jax.random.normal(ks[6], (H, SF), dtype=jnp.float32) * std}
    _L0_ffn_all = _L0_ffn_setup()
    _L0_ffn_in = {k: v for k, v in _L0_ffn_all.items() if k in ('router_w', 'gate_up_proj', 'down_proj', 'shared_gate_w', 'shared_up_w', 'shared_down_w')}
    del _L0_ffn_all

    def _L1_attn_setup():
        import jax, jax.numpy as jnp
        import numpy as np
        H = 16
        EPS = 1e-06
        key = jax.random.key(seed)
        ks = jax.random.split(key, 5)
        B, N, D = (4, 512, 128)
        x = jax.random.normal(ks[0], (B, N, D), dtype=jnp.float32)
        q = jax.random.normal(ks[1], (D,), dtype=jnp.float32)
        k = jax.random.normal(ks[2], (D,), dtype=jnp.float32)
        log_decay = jax.random.normal(ks[3], (H,), dtype=jnp.float32)
        norm_weight = jnp.ones((D,), dtype=jnp.float32)
        o_w = jax.random.normal(ks[4], (D, D), dtype=jnp.float32) * 0.02
        return {'x': x, 'q': q, 'k': k, 'log_decay': log_decay, 'norm_weight': norm_weight, 'o_w': o_w}
    _L1_attn_all = _L1_attn_setup()
    _L1_attn_in = {k: v for k, v in _L1_attn_all.items() if k in ('q', 'k', 'log_decay', 'norm_weight', 'o_w')}
    del _L1_attn_all

    def _L1_xattn_setup():
        import jax, jax.numpy as jnp
        import numpy as np
        Q_DIM, KV_DIM = (128, 128)
        H, HD, KVC, QC, R = (16, 64, 32, 48, 64)
        LOOKBACK = 2
        B, LQ, LK = (4, 256, 64)

        def _rope(x, pos):
            r = x.shape[-1]
            half = r // 2
            inv = 1.0 / 10000.0 ** (jnp.arange(half, dtype=jnp.float32) / half)
            ang = pos[..., None].astype(jnp.float32) * inv
            cos, sin = (jnp.cos(ang), jnp.sin(ang))
            x1, x2 = (x[..., :half], x[..., half:])
            return jnp.concatenate([x1 * cos - x2 * sin, x1 * sin + x2 * cos], axis=-1)
        key = jax.random.key(seed)
        ks = jax.random.split(key, 11)
        w = lambda k, shape: jax.random.normal(k, shape, jnp.float32) / np.sqrt(shape[0]).astype(np.float32)
        return {'q': jax.random.normal(ks[0], (B, LQ, Q_DIM), jnp.float32), 'kv': jax.random.normal(ks[1], (B, LK, KV_DIM), jnp.float32), 'seg_id': jnp.sort(jax.random.randint(ks[2], (B, LQ), 0, LK), axis=-1), 'w_kv_comp': w(ks[3], (KV_DIM, KVC)), 'w_q_down': w(ks[4], (Q_DIM, QC)), 'w_q_up': w(ks[5], (QC, H * HD)), 'w_q_rope': w(ks[6], (QC, H * R)), 'w_k_up': w(ks[7], (KVC, H * HD)), 'w_k_rope': w(ks[8], (KVC, R)), 'w_v_up': w(ks[9], (KVC, H * HD)), 'w_out': w(ks[10], (H * HD, Q_DIM))}
    _L1_xattn_all = _L1_xattn_setup()
    _L1_xattn_in = {k: v for k, v in _L1_xattn_all.items() if k in ('w_kv_comp', 'w_q_down', 'w_q_up', 'w_q_rope', 'w_k_up', 'w_k_rope', 'w_v_up', 'w_out')}
    del _L1_xattn_all

    def _L1_ffn_setup():
        import jax, jax.numpy as jnp
        import numpy as np
        NUM_EXPERTS = 8
        HIDDEN = 128
        INTER = 128
        BATCH = 2
        SEQ = 128
        TOP_K = 2
        SWIGLU_ALPHA = 1.702
        LIMIT = 7.0

        def _grouped_mm(x, w, expert_ids):
            onehot = jax.nn.one_hot(expert_ids, w.shape[0], dtype=x.dtype)
            y_all = jnp.einsum('tk,ekn->etn', x, w)
            return jnp.einsum('te,etn->tn', onehot, y_all)

        def _gpt_oss_swiglu(x):
            gate = jnp.minimum(x[..., ::2], LIMIT)
            up = jnp.clip(x[..., 1::2], -LIMIT, LIMIT)
            glu = gate * jax.nn.sigmoid(gate * SWIGLU_ALPHA)
            return (up + 1.0) * glu
        key = jax.random.key(seed)
        ks = jax.random.split(key, 7)
        hidden_states = jax.random.normal(ks[0], (BATCH, SEQ, HIDDEN), jnp.float32)
        router_indices = jax.random.randint(ks[1], (BATCH * SEQ, TOP_K), 0, NUM_EXPERTS)
        routing_weights = jax.nn.softmax(jax.random.normal(ks[2], (BATCH * SEQ, NUM_EXPERTS), jnp.float32), axis=-1)
        scale = 0.02
        gate_up_proj = jax.random.normal(ks[3], (NUM_EXPERTS, HIDDEN, 2 * INTER), jnp.float32) * scale
        gate_up_proj_bias = jax.random.normal(ks[4], (NUM_EXPERTS, 2 * INTER), jnp.float32) * scale
        down_proj = jax.random.normal(ks[5], (NUM_EXPERTS, INTER, HIDDEN), jnp.float32) * scale
        down_proj_bias = jax.random.normal(ks[6], (NUM_EXPERTS, HIDDEN), jnp.float32) * scale
        return {'hidden_states': hidden_states, 'router_indices': router_indices, 'routing_weights': routing_weights, 'gate_up_proj': gate_up_proj, 'gate_up_proj_bias': gate_up_proj_bias, 'down_proj': down_proj, 'down_proj_bias': down_proj_bias}
    _L1_ffn_all = _L1_ffn_setup()
    _L1_ffn_in = {k: v for k, v in _L1_ffn_all.items() if k in ('router_indices', 'routing_weights', 'gate_up_proj', 'gate_up_proj_bias', 'down_proj', 'down_proj_bias')}
    del _L1_ffn_all

    def _L2_attn_setup():
        import jax, jax.numpy as jnp
        import numpy as np
        import math
        D_MODEL = 128
        N_HEADS = 16
        HEAD_DIM = D_MODEL // N_HEADS

        def alibi_slopes(n_heads: int) -> jnp.ndarray:

            def pow2_slopes(n):
                start = 2 ** (-2 ** (-(math.log2(n) - 3)))
                return [start * start ** i for i in range(n)]
            if math.log2(n_heads).is_integer():
                s = pow2_slopes(n_heads)
            else:
                c = 2 ** math.floor(math.log2(n_heads))
                s = pow2_slopes(c)
                s.extend(pow2_slopes(2 * c)[0::2][:n_heads - c])
            return jnp.array(s, dtype=jnp.float32)
        key = jax.random.key(seed)
        ks = jax.random.split(key, 5)
        B, T, C = (2, 256, D_MODEL)
        std = 1.0 / math.sqrt(C)
        return {'x': jax.random.normal(ks[0], (B, T, C), dtype=jnp.float32), 'Wq': jax.random.normal(ks[1], (C, C), dtype=jnp.float32) * std, 'bq': jnp.zeros((C,), dtype=jnp.float32), 'Wk': jax.random.normal(ks[2], (C, C), dtype=jnp.float32) * std, 'bk': jnp.zeros((C,), dtype=jnp.float32), 'Wv': jax.random.normal(ks[3], (C, C), dtype=jnp.float32) * std, 'bv': jnp.zeros((C,), dtype=jnp.float32), 'Wo': jax.random.normal(ks[4], (C, C), dtype=jnp.float32) * std, 'bo': jnp.zeros((C,), dtype=jnp.float32)}
    _L2_attn_all = _L2_attn_setup()
    _L2_attn_in = {k: v for k, v in _L2_attn_all.items() if k in ('Wq', 'bq', 'Wk', 'bk', 'Wv', 'bv', 'Wo', 'bo')}
    del _L2_attn_all

    def _L2_xattn_setup():
        import jax, jax.numpy as jnp
        import numpy as np
        D_MODEL = 128
        NUM_HEADS = 16
        D_K = D_MODEL // NUM_HEADS
        key = jax.random.key(seed)
        ks = jax.random.split(key, 11)
        B, S = (2, 256)
        scale = 1.0 / np.sqrt(D_MODEL)
        inp = {'q': jax.random.normal(ks[0], (B, S, D_MODEL), jnp.float32), 'k': jax.random.normal(ks[1], (B, S, D_MODEL), jnp.float32), 'v': jax.random.normal(ks[2], (B, S, D_MODEL), jnp.float32), 'Wq': jax.random.normal(ks[3], (D_MODEL, D_MODEL), jnp.float32) * scale, 'bq': jnp.zeros((D_MODEL,), jnp.float32), 'Wk': jax.random.normal(ks[4], (D_MODEL, D_MODEL), jnp.float32) * scale, 'bk': jnp.zeros((D_MODEL,), jnp.float32), 'Wv': jax.random.normal(ks[5], (D_MODEL, D_MODEL), jnp.float32) * scale, 'bv': jnp.zeros((D_MODEL,), jnp.float32), 'Wo': jax.random.normal(ks[6], (D_MODEL, D_MODEL), jnp.float32) * scale, 'bo': jnp.zeros((D_MODEL,), jnp.float32)}
        return inp
    _L2_xattn_all = _L2_xattn_setup()
    _L2_xattn_in = {k: v for k, v in _L2_xattn_all.items() if k in ('Wq', 'bq', 'Wk', 'bk', 'Wv', 'bv', 'Wo', 'bo')}
    del _L2_xattn_all

    def _L2_ffn_setup():
        import jax, jax.numpy as jnp
        import numpy as np
        EPS = 1e-05

        def layernorm(x, w, b):
            mu = jnp.mean(x, axis=-1, keepdims=True)
            var = jnp.mean(jnp.square(x - mu), axis=-1, keepdims=True)
            return (x - mu) * jax.lax.rsqrt(var + EPS) * w + b

        def act_quant_fake(x):
            scale = 127.0 / jnp.clip(jnp.max(jnp.abs(x), axis=-1, keepdims=True), EPS, None)
            return jnp.clip(jnp.round(x * scale), -128.0, 127.0) / scale

        def weight_quant_fake(w):
            scale = 1.0 / jnp.clip(jnp.mean(jnp.abs(w)), EPS, None)
            return jnp.clip(jnp.round(w * scale), -1.0, 1.0) / scale

        def bitlinear(x, w, b):
            dqx = x + jax.lax.stop_gradient(act_quant_fake(x) - x)
            dqw = w + jax.lax.stop_gradient(weight_quant_fake(w) - w)
            return jnp.einsum('btd,hd->bth', dqx, dqw) + b
        key = jax.random.key(seed)
        ks = jax.random.split(key, 5)
        dim, hidden = (128, 512)
        B, T = (8, 256)
        return {'x': jax.random.normal(ks[0], (B, T, dim), dtype=jnp.float32), 'ln1_w': jnp.ones((dim,), jnp.float32), 'ln1_b': jnp.zeros((dim,), jnp.float32), 'w1': jax.random.normal(ks[1], (hidden, dim), jnp.float32) * (1.0 / np.sqrt(dim)), 'b1': jax.random.normal(ks[2], (hidden,), jnp.float32) * 0.01, 'ln2_w': jnp.ones((hidden,), jnp.float32), 'ln2_b': jnp.zeros((hidden,), jnp.float32), 'w2': jax.random.normal(ks[3], (dim, hidden), jnp.float32) * (1.0 / np.sqrt(hidden)), 'b2': jax.random.normal(ks[4], (dim,), jnp.float32) * 0.01}
    _L2_ffn_all = _L2_ffn_setup()
    _L2_ffn_in = {k: v for k, v in _L2_ffn_all.items() if k in ('ln1_w', 'ln1_b', 'w1', 'b1', 'ln2_w', 'ln2_b', 'w2', 'b2')}
    del _L2_ffn_all

    def _L3_attn_setup():
        import jax, jax.numpy as jnp
        import numpy as np
        NUM_HEADS = 16
        HIDDEN = 128
        ATTN_DIM = 64
        HEAD_OUT = 64
        OUT_DIM = 128
        BATCH, SEQ = (2, 256)

        def _split_heads(y, h):
            b, s, _ = y.shape
            return y.reshape(b, s, h, -1).transpose(0, 2, 1, 3)
        key = jax.random.key(seed)
        ks = jax.random.split(key, 9)
        s_in = 1.0 / np.sqrt(HIDDEN)
        s_o = 1.0 / np.sqrt(NUM_HEADS * HEAD_OUT)
        return {'x': jax.random.normal(ks[0], (BATCH, SEQ, HIDDEN), dtype=jnp.float32), 'Wq': jax.random.uniform(ks[1], (HIDDEN, NUM_HEADS * ATTN_DIM), jnp.float32, -s_in, s_in), 'bq': jax.random.uniform(ks[2], (NUM_HEADS * ATTN_DIM,), jnp.float32, -s_in, s_in), 'Wk': jax.random.uniform(ks[3], (HIDDEN, NUM_HEADS * ATTN_DIM), jnp.float32, -s_in, s_in), 'bk': jax.random.uniform(ks[4], (NUM_HEADS * ATTN_DIM,), jnp.float32, -s_in, s_in), 'Wv': jax.random.uniform(ks[5], (HIDDEN, NUM_HEADS * HEAD_OUT), jnp.float32, -s_in, s_in), 'bv': jax.random.uniform(ks[6], (HIDDEN, NUM_HEADS * HEAD_OUT)[1:], jnp.float32, -s_in, s_in), 'Wo': jax.random.uniform(ks[7], (NUM_HEADS * HEAD_OUT, OUT_DIM), jnp.float32, -s_o, s_o), 'bo': jax.random.uniform(ks[8], (OUT_DIM,), jnp.float32, -s_o, s_o)}
    _L3_attn_all = _L3_attn_setup()
    _L3_attn_in = {k: v for k, v in _L3_attn_all.items() if k in ('Wq', 'bq', 'Wk', 'bk', 'Wv', 'bv', 'Wo', 'bo')}
    del _L3_attn_all

    def _L3_xattn_setup():
        import jax, jax.numpy as jnp
        import numpy as np
        D_MODEL = 128
        NUM_HEADS = 16
        HEAD_DIM = D_MODEL // NUM_HEADS
        BATCH = 8
        SEQ = 256
        LN_EPS = 1e-05
        rng = jax.random.key(seed)
        ks = jax.random.split(rng, 16)
        s = 0.02
        w = lambda k: jax.random.normal(k, (D_MODEL, D_MODEL), jnp.float32) * s
        return {'query': jax.random.normal(ks[0], (BATCH, SEQ, D_MODEL), jnp.float32), 'key': jax.random.normal(ks[1], (BATCH, SEQ, D_MODEL), jnp.float32), 'value': jax.random.normal(ks[2], (BATCH, SEQ, D_MODEL), jnp.float32), 'Wq': w(ks[3]), 'bq': jnp.zeros((D_MODEL,), jnp.float32), 'Wk': w(ks[4]), 'bk': jnp.zeros((D_MODEL,), jnp.float32), 'Wv': w(ks[5]), 'bv': jnp.zeros((D_MODEL,), jnp.float32), 'ln_g': jnp.ones((D_MODEL,), jnp.float32), 'ln_b': jnp.zeros((D_MODEL,), jnp.float32), 'Wo': w(ks[6]), 'bo': jnp.zeros((D_MODEL,), jnp.float32)}
    _L3_xattn_all = _L3_xattn_setup()
    _L3_xattn_in = {k: v for k, v in _L3_xattn_all.items() if k in ('Wq', 'bq', 'Wk', 'bk', 'Wv', 'bv', 'ln_g', 'ln_b', 'Wo', 'bo')}
    del _L3_xattn_all

    def _L3_ffn_setup():
        import jax, jax.numpy as jnp
        import numpy as np
        H = 128
        DFF = 512
        E_ROUTED = 7
        TOP_K = 2

        def _swiglu(flat, gate_w, up_w, down_w):
            g = flat @ gate_w.T
            up = flat @ up_w.T
            return jax.nn.silu(g) * up @ down_w.T
        key = jax.random.key(seed)
        ks = jax.random.split(key, 8)
        s = 0.02
        return {'x': jax.random.normal(ks[0], (4, 256, H), jnp.float32), 'shared_up': jax.random.normal(ks[1], (DFF, H), jnp.float32) * s, 'shared_gate': jax.random.normal(ks[2], (DFF, H), jnp.float32) * s, 'shared_down': jax.random.normal(ks[3], (H, DFF), jnp.float32) * s, 'routed_up': jax.random.normal(ks[4], (E_ROUTED, DFF, H), jnp.float32) * s, 'routed_gate': jax.random.normal(ks[5], (E_ROUTED, DFF, H), jnp.float32) * s, 'routed_down': jax.random.normal(ks[6], (E_ROUTED, H, DFF), jnp.float32) * s, 'router_w': jax.random.normal(ks[7], (E_ROUTED, H), jnp.float32) * 0.02}
    _L3_ffn_all = _L3_ffn_setup()
    _L3_ffn_in = {k: v for k, v in _L3_ffn_all.items() if k in ('shared_up', 'shared_gate', 'shared_down', 'routed_up', 'routed_gate', 'routed_down', 'router_w')}
    del _L3_ffn_all
    return {'x': x, 'ctx_1024': ctx_1024, 'itok_BxS_0_511': itok_BxS_0_511, 'L0_attn_W_Q': _L0_attn_in['W_Q'], 'L0_attn_W_K': _L0_attn_in['W_K'], 'L0_attn_W_V': _L0_attn_in['W_V'], 'L0_attn_W_G': _L0_attn_in['W_G'], 'L0_attn_W_O': _L0_attn_in['W_O'], 'L0_attn_gn_weight': _L0_attn_in['gn_weight'], 'L0_attn_gn_bias': _L0_attn_in['gn_bias'], 'L0_xattn_w_q': _L0_xattn_in['w_q'], 'L0_xattn_w_kv': _L0_xattn_in['w_kv'], 'L0_xattn_w_concat': _L0_xattn_in['w_concat'], 'L0_ffn_router_w': _L0_ffn_in['router_w'], 'L0_ffn_gate_up_proj': _L0_ffn_in['gate_up_proj'], 'L0_ffn_down_proj': _L0_ffn_in['down_proj'], 'L0_ffn_shared_gate_w': _L0_ffn_in['shared_gate_w'], 'L0_ffn_shared_up_w': _L0_ffn_in['shared_up_w'], 'L0_ffn_shared_down_w': _L0_ffn_in['shared_down_w'], 'L1_attn_q': _L1_attn_in['q'], 'L1_attn_k': _L1_attn_in['k'], 'L1_attn_log_decay': _L1_attn_in['log_decay'], 'L1_attn_norm_weight': _L1_attn_in['norm_weight'], 'L1_attn_o_w': _L1_attn_in['o_w'], 'L1_xattn_w_kv_comp': _L1_xattn_in['w_kv_comp'], 'L1_xattn_w_q_down': _L1_xattn_in['w_q_down'], 'L1_xattn_w_q_up': _L1_xattn_in['w_q_up'], 'L1_xattn_w_q_rope': _L1_xattn_in['w_q_rope'], 'L1_xattn_w_k_up': _L1_xattn_in['w_k_up'], 'L1_xattn_w_k_rope': _L1_xattn_in['w_k_rope'], 'L1_xattn_w_v_up': _L1_xattn_in['w_v_up'], 'L1_xattn_w_out': _L1_xattn_in['w_out'], 'L1_ffn_router_indices': _L1_ffn_in['router_indices'], 'L1_ffn_routing_weights': _L1_ffn_in['routing_weights'], 'L1_ffn_gate_up_proj': _L1_ffn_in['gate_up_proj'], 'L1_ffn_gate_up_proj_bias': _L1_ffn_in['gate_up_proj_bias'], 'L1_ffn_down_proj': _L1_ffn_in['down_proj'], 'L1_ffn_down_proj_bias': _L1_ffn_in['down_proj_bias'], 'L2_attn_Wq': _L2_attn_in['Wq'], 'L2_attn_bq': _L2_attn_in['bq'], 'L2_attn_Wk': _L2_attn_in['Wk'], 'L2_attn_bk': _L2_attn_in['bk'], 'L2_attn_Wv': _L2_attn_in['Wv'], 'L2_attn_bv': _L2_attn_in['bv'], 'L2_attn_Wo': _L2_attn_in['Wo'], 'L2_attn_bo': _L2_attn_in['bo'], 'L2_xattn_Wq': _L2_xattn_in['Wq'], 'L2_xattn_bq': _L2_xattn_in['bq'], 'L2_xattn_Wk': _L2_xattn_in['Wk'], 'L2_xattn_bk': _L2_xattn_in['bk'], 'L2_xattn_Wv': _L2_xattn_in['Wv'], 'L2_xattn_bv': _L2_xattn_in['bv'], 'L2_xattn_Wo': _L2_xattn_in['Wo'], 'L2_xattn_bo': _L2_xattn_in['bo'], 'L2_ffn_ln1_w': _L2_ffn_in['ln1_w'], 'L2_ffn_ln1_b': _L2_ffn_in['ln1_b'], 'L2_ffn_w1': _L2_ffn_in['w1'], 'L2_ffn_b1': _L2_ffn_in['b1'], 'L2_ffn_ln2_w': _L2_ffn_in['ln2_w'], 'L2_ffn_ln2_b': _L2_ffn_in['ln2_b'], 'L2_ffn_w2': _L2_ffn_in['w2'], 'L2_ffn_b2': _L2_ffn_in['b2'], 'L3_attn_Wq': _L3_attn_in['Wq'], 'L3_attn_bq': _L3_attn_in['bq'], 'L3_attn_Wk': _L3_attn_in['Wk'], 'L3_attn_bk': _L3_attn_in['bk'], 'L3_attn_Wv': _L3_attn_in['Wv'], 'L3_attn_bv': _L3_attn_in['bv'], 'L3_attn_Wo': _L3_attn_in['Wo'], 'L3_attn_bo': _L3_attn_in['bo'], 'L3_xattn_Wq': _L3_xattn_in['Wq'], 'L3_xattn_bq': _L3_xattn_in['bq'], 'L3_xattn_Wk': _L3_xattn_in['Wk'], 'L3_xattn_bk': _L3_xattn_in['bk'], 'L3_xattn_Wv': _L3_xattn_in['Wv'], 'L3_xattn_bv': _L3_xattn_in['bv'], 'L3_xattn_ln_g': _L3_xattn_in['ln_g'], 'L3_xattn_ln_b': _L3_xattn_in['ln_b'], 'L3_xattn_Wo': _L3_xattn_in['Wo'], 'L3_xattn_bo': _L3_xattn_in['bo'], 'L3_ffn_shared_up': _L3_ffn_in['shared_up'], 'L3_ffn_shared_gate': _L3_ffn_in['shared_gate'], 'L3_ffn_shared_down': _L3_ffn_in['shared_down'], 'L3_ffn_routed_up': _L3_ffn_in['routed_up'], 'L3_ffn_routed_gate': _L3_ffn_in['routed_gate'], 'L3_ffn_routed_down': _L3_ffn_in['routed_down'], 'L3_ffn_router_w': _L3_ffn_in['router_w']}

def reference(x, ctx_1024, itok_BxS_0_511, L0_attn_W_Q, L0_attn_W_K, L0_attn_W_V, L0_attn_W_G, L0_attn_W_O, L0_attn_gn_weight, L0_attn_gn_bias, L0_xattn_w_q, L0_xattn_w_kv, L0_xattn_w_concat, L0_ffn_router_w, L0_ffn_gate_up_proj, L0_ffn_down_proj, L0_ffn_shared_gate_w, L0_ffn_shared_up_w, L0_ffn_shared_down_w, L1_attn_q, L1_attn_k, L1_attn_log_decay, L1_attn_norm_weight, L1_attn_o_w, L1_xattn_w_kv_comp, L1_xattn_w_q_down, L1_xattn_w_q_up, L1_xattn_w_q_rope, L1_xattn_w_k_up, L1_xattn_w_k_rope, L1_xattn_w_v_up, L1_xattn_w_out, L1_ffn_router_indices, L1_ffn_routing_weights, L1_ffn_gate_up_proj, L1_ffn_gate_up_proj_bias, L1_ffn_down_proj, L1_ffn_down_proj_bias, L2_attn_Wq, L2_attn_bq, L2_attn_Wk, L2_attn_bk, L2_attn_Wv, L2_attn_bv, L2_attn_Wo, L2_attn_bo, L2_xattn_Wq, L2_xattn_bq, L2_xattn_Wk, L2_xattn_bk, L2_xattn_Wv, L2_xattn_bv, L2_xattn_Wo, L2_xattn_bo, L2_ffn_ln1_w, L2_ffn_ln1_b, L2_ffn_w1, L2_ffn_b1, L2_ffn_ln2_w, L2_ffn_ln2_b, L2_ffn_w2, L2_ffn_b2, L3_attn_Wq, L3_attn_bq, L3_attn_Wk, L3_attn_bk, L3_attn_Wv, L3_attn_bv, L3_attn_Wo, L3_attn_bo, L3_xattn_Wq, L3_xattn_bq, L3_xattn_Wk, L3_xattn_bk, L3_xattn_Wv, L3_xattn_bv, L3_xattn_ln_g, L3_xattn_ln_b, L3_xattn_Wo, L3_xattn_bo, L3_ffn_shared_up, L3_ffn_shared_gate, L3_ffn_shared_down, L3_ffn_routed_up, L3_ffn_routed_gate, L3_ffn_routed_down, L3_ffn_router_w):
    import jax
    import jax.numpy as jnp

    def _L0_attn_ref(X, W_Q, W_K, W_V, W_G, W_O, gn_weight, gn_bias):
        import math
        import jax, jax.numpy as jnp
        import numpy as np
        B, L, DIM, HEADS = (4, 256, 128, 8)
        HEAD = DIM // HEADS
        SCALE_BASE = 512.0
        EPS = 1e-05

        def _xpos(x, downscale=False):
            l, dh = (x.shape[-2], x.shape[-1])
            half = dh // 2
            pos = jnp.arange(l, dtype=x.dtype)
            base = (jnp.arange(0, dh, 2, dtype=x.dtype) + 0.4 * dh) / (1.4 * dh)
            scale = base[None, :] ** (pos[:, None] / SCALE_BASE)
            inv_freq = 1.0 / 10000.0 ** (jnp.arange(half, dtype=x.dtype) / half)
            sinusoid = pos[:, None] * inv_freq[None, :]
            sin, cos = (jnp.sin(sinusoid), jnp.cos(sinusoid))
            if downscale:
                scale = 1.0 / scale
            s = jnp.repeat(sin * scale, 2, axis=-1)
            c = jnp.repeat(cos * scale, 2, axis=-1)
            x1, x2 = (x[..., ::2], x[..., 1::2])
            rot = jnp.stack([-x2, x1], axis=-1).reshape(x.shape)
            return x * c + rot * s

        def _decay_mask(l, gammas):
            n = jnp.arange(l)[:, None]
            m = jnp.arange(l)[None, :]
            lg = jnp.log(gammas)
            expo = (n - m).astype(jnp.float32)[None, :, :] * lg[:, None, None]
            return jnp.where((n >= m)[None], jnp.exp(expo), 0.0)
        b, l, d = X.shape
        h = W_Q.shape[0]
        gammas = 1.0 - jnp.exp(jnp.linspace(math.log(1.0 / 32.0), math.log(1.0 / 512.0), h)).astype(jnp.float32)
        Q = jnp.einsum('bld,hde->bhle', X, W_Q)
        K = jnp.einsum('bld,hde->bhle', X, W_K)
        V = jnp.einsum('bld,hdv->bhlv', X, W_V)
        Q = _xpos(Q)
        K = _xpos(K, downscale=True)
        D = _decay_mask(l, gammas).astype(X.dtype)
        scores = jnp.einsum('bhle,bhme->bhlm', Q, K) * D[None]
        Y = jnp.einsum('bhlm,bhmv->bhlv', scores, V)
        mean = Y.mean(axis=-1, keepdims=True)
        var = Y.var(axis=-1, keepdims=True)
        Yn = (Y - mean) * jax.lax.rsqrt(var + EPS)
        Yn = jnp.transpose(Yn, (0, 2, 1, 3)).reshape(b, l, -1)
        Yn = Yn * gn_weight + gn_bias
        G = X @ W_G
        out = G * jax.nn.sigmoid(G) * Yn @ W_O
        return out

    def _L0_xattn_ref(q, kv, mem, w_q, w_kv, w_concat):
        import jax, jax.numpy as jnp
        import numpy as np
        D_MODEL = 128
        N_HEAD = 16
        D_HEAD = D_MODEL // N_HEAD
        B, L, D = q.shape
        c = jnp.concatenate([mem, kv], axis=1)
        qh = (q @ w_q).reshape(B, L, N_HEAD, D_HEAD).transpose(0, 2, 1, 3)
        kvp = c @ w_kv
        k, v = (kvp[..., :D_HEAD], kvp[..., D_HEAD:])
        attn_score = jnp.einsum('bhid,bjd->bhij', qh, k) / np.sqrt(D_HEAD)
        attn_prob = jax.nn.softmax(attn_score, axis=-1)
        out = jnp.einsum('bhij,bjd->bhid', attn_prob, v)
        out = out.transpose(0, 2, 1, 3).reshape(B, L, D)
        return out @ w_concat

    def _L0_ffn_ref(hidden_states, router_w, gate_up_proj, down_proj, shared_gate_w, shared_up_w, shared_down_w):
        import jax, jax.numpy as jnp
        import numpy as np
        B, S, H = (2, 256, 128)
        N, F, SF, K = (16, 128, 512, 1)
        b, s, h = hidden_states.shape
        hidden = hidden_states.reshape(-1, h)
        t = hidden.shape[0]
        logits = hidden @ router_w.T
        top_vals, top_idx = jax.lax.top_k(logits, K)
        scores = jnp.full_like(logits, -jnp.inf)
        scores = scores.at[jnp.arange(t)[:, None], top_idx].set(top_vals)
        scores = jax.nn.sigmoid(scores.astype(jnp.float32)).astype(hidden.dtype)
        routed_in = hidden[None, :, :] * scores.T[:, :, None]
        gate_up = jnp.einsum('nth,nhf->ntf', routed_in, gate_up_proj)
        gate, up = jnp.split(gate_up, 2, axis=-1)
        routed_out = jnp.einsum('ntf,nfh->nth', up * jax.nn.silu(gate), down_proj)
        expert_sum = routed_out.sum(axis=0)
        shared = jax.nn.silu(hidden @ shared_gate_w.T) * (hidden @ shared_up_w.T) @ shared_down_w.T
        return (shared + expert_sum).reshape(b, s, h)

    def _L1_attn_ref(x, q, k, log_decay, norm_weight, o_w):
        import jax, jax.numpy as jnp
        import numpy as np
        H = 16
        EPS = 1e-06
        b, n, dm = x.shape
        dh = dm // H
        qh = q.reshape(H, dh)
        kh = k.reshape(H, dh)
        v = x.reshape(b, n, H, dh)
        lam = jax.nn.sigmoid(log_decay)

        def step(S, v_t):
            S = lam[None, :, None, None] * S + kh[None, :, :, None] * v_t[:, :, None, :]
            o_t = jnp.einsum('hd,bhdv->bhv', qh, S)
            return (S, o_t)
        S0 = jnp.zeros((b, H, dh, dh), dtype=x.dtype)
        _, o = jax.lax.scan(step, S0, jnp.moveaxis(v, 1, 0))
        o = jnp.moveaxis(o, 0, 1).reshape(b, n, dm)
        o = o * jax.lax.rsqrt(jnp.mean(o * o, axis=-1, keepdims=True) + EPS) * norm_weight
        return o @ o_w.T

    def _L1_xattn_ref(q, kv, seg_id, w_kv_comp, w_q_down, w_q_up, w_q_rope, w_k_up, w_k_rope, w_v_up, w_out):
        import jax, jax.numpy as jnp
        import numpy as np
        Q_DIM, KV_DIM = (128, 128)
        H, HD, KVC, QC, R = (16, 64, 32, 48, 64)
        LOOKBACK = 2
        B, LQ, LK = (4, 256, 64)

        def _rope(x, pos):
            r = x.shape[-1]
            half = r // 2
            inv = 1.0 / 10000.0 ** (jnp.arange(half, dtype=jnp.float32) / half)
            ang = pos[..., None].astype(jnp.float32) * inv
            cos, sin = (jnp.cos(ang), jnp.sin(ang))
            x1, x2 = (x[..., :half], x[..., half:])
            return jnp.concatenate([x1 * cos - x2 * sin, x1 * sin + x2 * cos], axis=-1)
        b, lq, _ = q.shape
        lk = kv.shape[1]
        kv_c = kv @ w_kv_comp
        qc = q @ w_q_down
        q_nope = (qc @ w_q_up).reshape(b, lq, H, HD)
        q_rope = (qc @ w_q_rope).reshape(b, lq, H, R)
        q_rope = _rope(q_rope, jnp.arange(lq)[None, :, None])
        k_nope = (kv_c @ w_k_up).reshape(b, lk, H, HD)
        k_rope = _rope(kv_c @ w_k_rope, jnp.arange(lk)[None, :])
        v = (kv_c @ w_v_up).reshape(b, lk, H, HD)
        scale = 1.0 / np.sqrt(HD + R).astype(np.float32)
        scores = (jnp.einsum('bqhd,bkhd->bhqk', q_nope, k_nope) + jnp.einsum('bqhr,bkr->bhqk', q_rope, k_rope)) * scale
        k_idx = jnp.arange(lk)[None, None, :]
        q_seg = seg_id[:, :, None]
        good = (k_idx <= q_seg) & (k_idx >= q_seg - LOOKBACK)
        neg = jnp.finfo(scores.dtype).min
        scores = jnp.where(good[:, None, :, :], scores, neg)
        attn = jax.nn.softmax(scores, axis=-1)
        out = jnp.einsum('bhqk,bkhd->bqhd', attn, v).reshape(b, lq, H * HD)
        return out @ w_out

    def _L1_ffn_ref(hidden_states, router_indices, routing_weights, gate_up_proj, gate_up_proj_bias, down_proj, down_proj_bias):
        import jax, jax.numpy as jnp
        import numpy as np
        NUM_EXPERTS = 8
        HIDDEN = 128
        INTER = 128
        BATCH = 2
        SEQ = 128
        TOP_K = 2
        SWIGLU_ALPHA = 1.702
        LIMIT = 7.0

        def _grouped_mm(x, w, expert_ids):
            onehot = jax.nn.one_hot(expert_ids, w.shape[0], dtype=x.dtype)
            y_all = jnp.einsum('tk,ekn->etn', x, w)
            return jnp.einsum('te,etn->tn', onehot, y_all)

        def _gpt_oss_swiglu(x):
            gate = jnp.minimum(x[..., ::2], LIMIT)
            up = jnp.clip(x[..., 1::2], -LIMIT, LIMIT)
            glu = gate * jax.nn.sigmoid(gate * SWIGLU_ALPHA)
            return (up + 1.0) * glu
        B = hidden_states.shape[0]
        H = hidden_states.shape[-1]
        x = hidden_states.reshape(-1, H)
        M = x.shape[0]
        top_k = router_indices.shape[1]
        num_experts = gate_up_proj.shape[0]
        topk_weights = jnp.take_along_axis(routing_weights, router_indices, axis=1)
        flat_experts = router_indices.reshape(-1)
        sort_idx = jnp.argsort(flat_experts)
        sorted_pos = sort_idx // top_k
        expert_sorted = flat_experts[sort_idx]
        grouped = x[sorted_pos]
        gate_up = _grouped_mm(grouped, gate_up_proj, expert_sorted)
        gate_up = gate_up + gate_up_proj_bias[expert_sorted]
        inter = _gpt_oss_swiglu(gate_up)
        down = _grouped_mm(inter, down_proj, expert_sorted)
        down = down + down_proj_bias[expert_sorted]
        down = down * topk_weights.reshape(-1)[sort_idx][:, None]
        out = jnp.zeros((M, H), x.dtype).at[sorted_pos].add(down)
        return out.reshape(B, -1, H)

    def _L2_attn_ref(x, Wq, bq, Wk, bk, Wv, bv, Wo, bo):
        import jax, jax.numpy as jnp
        import numpy as np
        import math
        D_MODEL = 128
        N_HEADS = 16
        HEAD_DIM = D_MODEL // N_HEADS

        def alibi_slopes(n_heads: int) -> jnp.ndarray:

            def pow2_slopes(n):
                start = 2 ** (-2 ** (-(math.log2(n) - 3)))
                return [start * start ** i for i in range(n)]
            if math.log2(n_heads).is_integer():
                s = pow2_slopes(n_heads)
            else:
                c = 2 ** math.floor(math.log2(n_heads))
                s = pow2_slopes(c)
                s.extend(pow2_slopes(2 * c)[0::2][:n_heads - c])
            return jnp.array(s, dtype=jnp.float32)
        B, T, C = x.shape
        H, D = (N_HEADS, HEAD_DIM)
        scale = D ** (-0.5)
        q = (x @ Wq + bq).reshape(B, T, H, D).transpose(0, 2, 1, 3)
        k = (x @ Wk + bk).reshape(B, T, H, D).transpose(0, 2, 1, 3)
        v = (x @ Wv + bv).reshape(B, T, H, D).transpose(0, 2, 1, 3)
        scores = jnp.einsum('bhqd,bhkd->bhqk', q, k) * scale
        pos = (jnp.arange(T)[:, None] - jnp.arange(T)[None, :]).astype(jnp.float32)
        bias = alibi_slopes(H)[:, None, None] * pos
        scores = scores + bias[None]
        causal = jnp.tril(jnp.ones((T, T), dtype=bool))
        scores = jnp.where(causal, scores, -jnp.inf)
        attn = jax.nn.softmax(scores, axis=-1)
        out = jnp.einsum('bhqk,bhkd->bhqd', attn, v)
        out = out.transpose(0, 2, 1, 3).reshape(B, T, C)
        return out @ Wo + bo

    def _L2_xattn_ref(q, k, v, Wq, bq, Wk, bk, Wv, bv, Wo, bo):
        import jax, jax.numpy as jnp
        import numpy as np
        D_MODEL = 128
        NUM_HEADS = 16
        D_K = D_MODEL // NUM_HEADS
        B, S, _ = q.shape
        H, Dk = (NUM_HEADS, D_K)

        def proj(x, W, b):
            y = x @ W + b
            return y.reshape(B, -1, H, Dk).transpose(0, 2, 1, 3)
        qh = proj(q, Wq, bq)
        kh = proj(k, Wk, bk)
        vh = proj(v, Wv, bv)
        scores = jnp.einsum('bhqd,bhkd->bhqk', qh, kh) / jnp.sqrt(jnp.float32(Dk))
        weights = jax.nn.softmax(scores, axis=-1)
        x = jnp.einsum('bhqk,bhkd->bhqd', weights, vh)
        x = x.transpose(0, 2, 1, 3).reshape(B, S, D_MODEL)
        return x @ Wo + bo

    def _L2_ffn_ref(x, ln1_w, ln1_b, w1, b1, ln2_w, ln2_b, w2, b2):
        import jax, jax.numpy as jnp
        import numpy as np
        EPS = 1e-05

        def layernorm(x, w, b):
            mu = jnp.mean(x, axis=-1, keepdims=True)
            var = jnp.mean(jnp.square(x - mu), axis=-1, keepdims=True)
            return (x - mu) * jax.lax.rsqrt(var + EPS) * w + b

        def act_quant_fake(x):
            scale = 127.0 / jnp.clip(jnp.max(jnp.abs(x), axis=-1, keepdims=True), EPS, None)
            return jnp.clip(jnp.round(x * scale), -128.0, 127.0) / scale

        def weight_quant_fake(w):
            scale = 1.0 / jnp.clip(jnp.mean(jnp.abs(w)), EPS, None)
            return jnp.clip(jnp.round(w * scale), -1.0, 1.0) / scale

        def bitlinear(x, w, b):
            dqx = x + jax.lax.stop_gradient(act_quant_fake(x) - x)
            dqw = w + jax.lax.stop_gradient(weight_quant_fake(w) - w)
            return jnp.einsum('btd,hd->bth', dqx, dqw) + b
        h = layernorm(x, ln1_w, ln1_b)
        h = bitlinear(h, w1, b1)
        h = jax.nn.gelu(h, approximate=False)
        h = layernorm(h, ln2_w, ln2_b)
        out = bitlinear(h, w2, b2)
        return out

    def _L3_attn_ref(x, Wq, bq, Wk, bk, Wv, bv, Wo, bo):
        import jax, jax.numpy as jnp
        import numpy as np
        NUM_HEADS = 16
        HIDDEN = 128
        ATTN_DIM = 64
        HEAD_OUT = 64
        OUT_DIM = 128
        BATCH, SEQ = (2, 256)

        def _split_heads(y, h):
            b, s, _ = y.shape
            return y.reshape(b, s, h, -1).transpose(0, 2, 1, 3)
        h = NUM_HEADS
        q = _split_heads(x @ Wq + bq, h)
        k = _split_heads(x @ Wk + bk, h)
        v = _split_heads(x @ Wv + bv, h)
        scale = 1.0 / jnp.sqrt(jnp.float32(ATTN_DIM))
        pattern = jnp.einsum('bhid,bhjd->bhij', k, q) * scale
        prob = jax.nn.softmax(pattern, axis=-2)
        out = jnp.einsum('bhis,bhid->bhsd', prob, v)
        b, _, s, dv = out.shape
        concat = out.transpose(0, 2, 1, 3).reshape(b, s, h * dv)
        return concat @ Wo + bo

    def _L3_xattn_ref(query, key, value, Wq, bq, Wk, bk, Wv, bv, ln_g, ln_b, Wo, bo):
        import jax, jax.numpy as jnp
        import numpy as np
        D_MODEL = 128
        NUM_HEADS = 16
        HEAD_DIM = D_MODEL // NUM_HEADS
        BATCH = 8
        SEQ = 256
        LN_EPS = 1e-05
        N, L, dm = query.shape
        H, Dh = (NUM_HEADS, HEAD_DIM)
        q = (query @ Wq.T + bq).reshape(N, L, H, Dh).transpose(0, 2, 1, 3)
        k = (key @ Wk.T + bk).reshape(N, L, H, Dh).transpose(0, 2, 1, 3)
        v = (value @ Wv.T + bv).reshape(N, L, H, Dh).transpose(0, 2, 1, 3)
        energy = jnp.einsum('nhld,ngld->nlhg', q, k)
        attn = jax.nn.softmax(energy / jnp.sqrt(jnp.float32(dm)), axis=3)
        out = jnp.einsum('nlhg,ngld->nhld', attn, v)
        out = out.transpose(0, 2, 1, 3).reshape(N, L, dm)
        mu = out.mean(axis=-1, keepdims=True)
        var = out.var(axis=-1, keepdims=True)
        out = (out - mu) / jnp.sqrt(var + LN_EPS) * ln_g + ln_b
        return out @ Wo.T + bo

    def _L3_ffn_ref(x, shared_up, shared_gate, shared_down, routed_up, routed_gate, routed_down, router_w):
        import jax, jax.numpy as jnp
        import numpy as np
        H = 128
        DFF = 512
        E_ROUTED = 7
        TOP_K = 2

        def _swiglu(flat, gate_w, up_w, down_w):
            g = flat @ gate_w.T
            up = flat @ up_w.T
            return jax.nn.silu(g) * up @ down_w.T
        orig_shape = x.shape
        flat = x.reshape(-1, H)
        out = _swiglu(flat, shared_gate, shared_up, shared_down)
        logits = flat @ router_w.T
        probs = jax.nn.softmax(logits, axis=-1)
        top_vals, top_idx = jax.lax.top_k(probs, TOP_K)
        top_vals = top_vals / (top_vals.sum(-1, keepdims=True) + 1e-09)
        combine = jnp.sum(jax.nn.one_hot(top_idx, E_ROUTED, dtype=flat.dtype) * top_vals[..., None], axis=1)
        routed = jnp.zeros_like(flat)
        for e in range(E_ROUTED):
            eo = _swiglu(flat, routed_gate[e], routed_up[e], routed_down[e])
            routed = routed + combine[:, e:e + 1] * eo
        return (out + routed).reshape(orig_shape)
    x = x + _L0_attn_ref(_layernorm(x, axis=-1), L0_attn_W_Q, L0_attn_W_K, L0_attn_W_V, L0_attn_W_G, L0_attn_W_O, L0_attn_gn_weight, L0_attn_gn_bias)
    x = x + _L0_xattn_ref(_layernorm(x, axis=-1), ctx_1024, ctx_1024, L0_xattn_w_q, L0_xattn_w_kv, L0_xattn_w_concat)
    x = x + _L0_ffn_ref(_layernorm(x, axis=-1), L0_ffn_router_w, L0_ffn_gate_up_proj, L0_ffn_down_proj, L0_ffn_shared_gate_w, L0_ffn_shared_up_w, L0_ffn_shared_down_w)
    x = x + _L1_attn_ref(_layernorm(x, axis=-1), L1_attn_q, L1_attn_k, L1_attn_log_decay, L1_attn_norm_weight, L1_attn_o_w)
    x = x + _L1_xattn_ref(_layernorm(x, axis=-1), ctx_1024, itok_BxS_0_511, L1_xattn_w_kv_comp, L1_xattn_w_q_down, L1_xattn_w_q_up, L1_xattn_w_q_rope, L1_xattn_w_k_up, L1_xattn_w_k_rope, L1_xattn_w_v_up, L1_xattn_w_out)
    x = x + _L1_ffn_ref(_layernorm(x, axis=-1), L1_ffn_router_indices, L1_ffn_routing_weights, L1_ffn_gate_up_proj, L1_ffn_gate_up_proj_bias, L1_ffn_down_proj, L1_ffn_down_proj_bias)
    x = x + _L2_attn_ref(_layernorm(x, axis=-1), L2_attn_Wq, L2_attn_bq, L2_attn_Wk, L2_attn_bk, L2_attn_Wv, L2_attn_bv, L2_attn_Wo, L2_attn_bo)
    x = x + _L2_xattn_ref(_layernorm(x, axis=-1), ctx_1024, ctx_1024, L2_xattn_Wq, L2_xattn_bq, L2_xattn_Wk, L2_xattn_bk, L2_xattn_Wv, L2_xattn_bv, L2_xattn_Wo, L2_xattn_bo)
    x = x + _L2_ffn_ref(_layernorm(x, axis=-1), L2_ffn_ln1_w, L2_ffn_ln1_b, L2_ffn_w1, L2_ffn_b1, L2_ffn_ln2_w, L2_ffn_ln2_b, L2_ffn_w2, L2_ffn_b2)
    x = x + _L3_attn_ref(_layernorm(x, axis=-1), L3_attn_Wq, L3_attn_bq, L3_attn_Wk, L3_attn_bk, L3_attn_Wv, L3_attn_bv, L3_attn_Wo, L3_attn_bo)
    x = x + _L3_xattn_ref(_layernorm(x, axis=-1), ctx_1024, ctx_1024, L3_xattn_Wq, L3_xattn_bq, L3_xattn_Wk, L3_xattn_bk, L3_xattn_Wv, L3_xattn_bv, L3_xattn_ln_g, L3_xattn_ln_b, L3_xattn_Wo, L3_xattn_bo)
    x = x + _L3_ffn_ref(_layernorm(x, axis=-1), L3_ffn_shared_up, L3_ffn_shared_gate, L3_ffn_shared_down, L3_ffn_routed_up, L3_ffn_routed_gate, L3_ffn_routed_down, L3_ffn_router_w)
    return x

_drawn_inputs = setup_inputs


def setup_inputs(seed=0):
    import zlib

    import numpy as np

    out = dict(_drawn_inputs(seed))
    spreads = {'L0_attn_gn_weight': (1.0, 0.6),
     'L0_attn_gn_bias': (0.0, 0.8),
     'L1_attn_norm_weight': (1.0, 0.2),
     'L2_attn_bq': (0.0, 0.606),
     'L2_attn_bk': (0.0, 0.8),
     'L2_attn_bv': (0.0, 0.1),
     'L2_attn_bo': (0.0, 0.1),
     'L2_xattn_bq': (0.0, 0.502),
     'L2_xattn_bk': (0.0, 0.8),
     'L2_xattn_bv': (0.0, 0.1),
     'L2_xattn_bo': (0.0, 0.1),
     'L2_ffn_ln1_w': (1.0, 0.2),
     'L2_ffn_ln1_b': (0.0, 0.1),
     'L2_ffn_ln2_w': (1.0, 0.2),
     'L2_ffn_ln2_b': (0.0, 0.1),
     'L3_xattn_bq': (0.0, 0.8),
     'L3_xattn_bk': (0.0, 0.8),
     'L3_xattn_bv': (0.0, 0.1),
     'L3_xattn_ln_g': (1.0, 0.6),
     'L3_xattn_ln_b': (0.0, 0.602),
     'L3_xattn_bo': (0.0, 0.1)}
    factors = {'L0_attn_W_Q': 8.0,
     'L0_attn_W_K': 8.0,
     'L0_attn_W_V': 8.0,
     'L0_attn_W_G': 8.0,
     'L0_attn_W_O': 8.0,
     'L0_ffn_router_w': 8.0,
     'L0_ffn_gate_up_proj': 8.0,
     'L0_ffn_down_proj': 8.0,
     'L0_ffn_shared_gate_w': 5.473,
     'L0_ffn_shared_up_w': 5.433,
     'L0_ffn_shared_down_w': 5.387,
     'L1_ffn_routing_weights': 8.0,
     'L1_ffn_gate_up_proj': 8.0,
     'L1_ffn_gate_up_proj_bias': 8.0,
     'L1_ffn_down_proj': 8.0,
     'L1_ffn_down_proj_bias': 8.0,
     'L2_ffn_b1': 6.802,
     'L2_ffn_b2': 8.0,
     'L3_attn_Wq': 8.0,
     'L3_attn_bq': 8.0,
     'L3_attn_Wk': 8.0,
     'L3_attn_bk': 8.0,
     'L3_attn_bv': 3.354,
     'L3_attn_bo': 5.374,
     'L3_xattn_Wq': 8.0,
     'L3_xattn_Wk': 8.0,
     'L3_ffn_shared_up': 8.0,
     'L3_ffn_shared_gate': 8.0,
     'L3_ffn_shared_down': 8.0,
     'L3_ffn_routed_up': 8.0,
     'L3_ffn_routed_gate': 8.0,
     'L3_ffn_routed_down': 8.0,
     'L3_ffn_router_w': 8.0}
    for name, (base, spread) in spreads.items():
        noise = np.random.default_rng([zlib.crc32(name.encode()), seed]).standard_normal(out[name].shape)
        drawn = base * np.exp(spread * noise) if base else spread * noise
        out[name] = jnp.asarray(drawn.astype(out[name].dtype))
    for name, factor in factors.items():
        out[name] = (out[name] * factor).astype(out[name].dtype)
    return out
```

```python
import math
from contextlib import ExitStack

import numpy as np
import concourse.bass as bass
from concourse import mybir

F32 = mybir.dt.float32
BF16 = mybir.dt.bfloat16
I32 = mybir.dt.int32
ALU = mybir.AluOpType
ACT = mybir.ActivationFunctionType
AX_X = mybir.AxisListType.X

B, L, D = 4, 256, 128
TOKENS = B * L
TILES = TOKENS // 128
HALVES = 2
MASKED = -1e30

WEIGHTS = {
    "l0_attn": dict(wq=(128, 256), wqs=(128, 256), wk=(128, 256), wks=(128, 256), wv=(128, 128), wg=(128, 128),
                    wo=(128, 128), gnw=(128, 1), gnb=(128, 1)),
    "l0_xattn": dict(wq=(128, 128), wk=(128, 8), wv=(128, 8), wo=(128, 128)),
    "l0_ffn": dict(router=(128, 16), gate_up=(128, 16 * 256), down=(128, 16 * 128),
                   s_gate=(128, 512), s_up=(128, 512), s_down=(128, 512)),
    "l1_attn": dict(q=(128, 1), k=(128, 1), log_decay=(128, 1), norm=(128, 1), wo=(128, 128), headsum=(128, 128)),
    "l1_xattn": dict(kv_comp=(128, 32), q_down=(128, 48), q_upT=(64, 16 * 48), q_rope=(48, 1024),
                     k_upT=(64, 16 * 32), k_rope=(32, 64), v_upT=(64, 16 * 32), out=(64, 16 * 128)),
    "l1_ffn": dict(gate=(128, 8 * 128), up=(128, 8 * 128), gate_b=(128, 8), up_b=(128, 8), down=(128, 8 * 128),
                   down_b=(8, 128), route_w=(128, 2 * 8)),
    "l2_attn": dict(wq=(128, 128), wk=(128, 128), wv=(128, 128), wo=(128, 128), bq=(128, 1), bk=(128, 1),
                    bv=(1, 128), bo=(1, 128)),
    "l2_xattn": dict(wq=(128, 128), wk=(128, 128), wv=(128, 128), wo=(128, 128), bq=(128, 1), bk=(128, 1),
                     bv=(1, 128), bo=(1, 128)),
    "l2_ffn": dict(w1=(128, 512), b1=(128, 512), w2=(128, 512), b2=(128, 128), ln1w=(128, 128), ln1b=(128, 128),
                   ln2w=(128, 512), ln2b=(128, 512)),
    "l3_attn": dict(wq=(128, 1024), wk=(128, 1024), wv=(128, 1024), wo=(128, 1024), bq=(128, 8), bk=(128, 8),
                    bv=(128, 8), bo=(1, 128)),
    "l3_xattn": dict(wq=(128, 128), wk=(128, 128), wv=(128, 128), wo=(128, 128), bq=(1, 128), bk=(1, 128),
                     bv=(1, 128), bo=(1, 128), ln_g=(128, 1), ln_b=(128, 1)),
    "l3_ffn": dict(router=(128, 7), gate=(128, 8 * 512), up=(128, 8 * 512), down=(128, 8 * 512)),
}
BLOCKS = list(WEIGHTS)


def columns(block):
    return sum(c for _, c in WEIGHTS[block].values())


def pack(block, parts):
    out = np.zeros((128, columns(block)), np.float32)
    at = 0
    for name, (rows, cols) in WEIGHTS[block].items():
        out[:rows, at:at + cols] = np.ascontiguousarray(parts[name]).reshape(rows, cols)
        at += cols
    return out


def bf16_bits(a):
    bits = np.ascontiguousarray(a, np.float32).view(np.uint32).astype(np.uint64)
    return ((bits + 0x7FFF + ((bits >> 16) & 1)) >> 16).astype(np.uint16)


def split3(a):
    a = np.asarray(a, np.float32)
    parts = []
    for _ in range(3):
        p = bf16_bits(a)
        parts.append(p)
        a = a - (p.astype(np.uint32) << 16).view(np.float32)
    return np.stack(parts)


CONST = dict(ident=128, tri3=384, cq=512, sq=512, ck=512, sk=512, iota16=16, iota8=8, key_index=6, rope_c=8 * 32, rope_s=8 * 32)


def constants():
    c = {}
    c["ident"] = np.eye(128)
    m, n = np.arange(128)[:, None], np.arange(128)[None, :]
    tri = (m <= n).astype(float)
    c["tri3"] = np.concatenate([tri, np.ones((128, 128)), tri], 1)
    heads, e = 8, 16
    pos = np.arange(L, dtype=float)
    base = (np.arange(0, e, 2) + 0.4 * e) / (1.4 * e)
    scale = base[None] ** (pos[:, None] / 512.0)
    ang = pos[:, None] / 10000.0 ** (np.arange(e // 2) / (e // 2))[None]
    gam = 1.0 - np.exp(np.linspace(math.log(1 / 32), math.log(1 / 512), heads))
    t = {k: np.zeros((128, 2, L)) for k in ("cq", "sq", "ck", "sk")}
    for h in range(heads):
        for i in range(e):
            r, g = 32 * (h % 4) + i, h // 4
            co, si = np.cos(ang[:, i // 2]), np.sin(ang[:, i // 2]) * (1 if i % 2 else -1)
            up, dn = scale[:, i // 2] * gam[h] ** (pos - 128), gam[h] ** (128 - pos) / scale[:, i // 2]
            t["cq"][r, g], t["sq"][r, g] = co * up, si * up
            t["ck"][r, g], t["sk"][r, g] = co * dn, si * dn
    for k, v in t.items():
        c[k] = v.reshape(128, -1)
    c["iota16"] = np.tile(16.0 - np.arange(16), (128, 1))
    c["iota8"] = np.tile(8.0 - np.arange(8), (128, 1))
    c["key_index"] = np.stack([np.arange(128) + 128 * kc + j for kc in range(2) for j in range(3)], 1)
    ang = pos[:, None] / 10000.0 ** (np.arange(32) / 32)[None]
    cos, sin = np.cos(ang), np.sin(ang)
    tile = lambda a: np.tile(a.reshape(2, 128, -1).transpose(1, 0, 2), (1, 4, 1)).reshape(128, -1)
    c["rope_c"], c["rope_s"] = tile(cos), tile(sin)
    return np.concatenate([c[k].reshape(128, w) for k, w in CONST.items()], 1).astype(np.float32)


def alibi_slopes():
    start = 2 ** (-2 ** (-(math.log2(16) - 3)))
    return np.array([start * start ** i for i in range(16)], np.float32)


def stack_constants():
    pos = np.tile(np.arange(L, dtype=np.float32), B)
    s = alibi_slopes().reshape(8, 2)
    qb = split3(s[:, :, None] * pos)
    kb = split3(-s[:, :, None] * pos)
    one = bf16_bits(np.ones((2, 3, 8, TOKENS)))
    q = np.concatenate([one, qb.transpose(2, 0, 1, 3)], 1)
    k = np.concatenate([kb.transpose(2, 0, 1, 3), one, one], 1)
    halves = lambda a: np.ascontiguousarray(a.reshape(2, -1, 8, HALVES, 512).transpose(0, 1, 3, 2, 4))
    return halves(q), halves(k)


def small_constants():
    m, n = np.arange(128)[:, None], np.arange(128)[None, :]
    parts = [np.eye(128), np.where(n <= m, 0.0, MASKED), np.where(m <= n, 0.0, MASKED), ((m % 64) < 3) * np.ones((128, 128))]
    sel = np.zeros((128, 16, 128))
    for e in range(16):
        for p in range(3):
            sel[32 * p + e, e, :] = 1.0
    return bf16_bits(np.concatenate(parts + [sel.reshape(128, -1)], 1))


class Order:

    def __init__(self, engine, done):
        self.engine, self.done, self.n = engine, done, 0

    def __call__(self, instruction):
        self.n += 1
        instruction.then_inc(self.done, 1)

    def settle(self):
        self.engine.wait_ge(self.done, self.n)


class Space:

    def __init__(self, tile, size):
        self.tile, self.size, self.at, self.most = tile, size, 0, 0

    def reset(self):
        self.at = 0

    def __call__(self, cols, dtype=F32):
        words = cols if dtype != BF16 else (cols + 1) // 2
        a = self.tile[:, self.at:self.at + words]
        self.at += words
        self.most = max(self.most, self.at)
        assert self.at <= self.size, (self.at, self.size)
        return a if dtype == F32 else a.bitcast(dtype)


class Core:
    pass


def bcast(ap, at, n):
    a = ap.unsqueeze(at)
    shape = list(a.shape)
    shape[at] = n
    return a.broadcast_to(shape)


def layernorm(c, k):
    nc = c.nc
    var_ready, rstd_ready, xn_ready = c.sem("ln_var_ready"), c.sem("ln_rstd_ready"), c.sem("xn_ready")
    xt_psum, xt_ready = c.sem("xt_psum"), c.sem("xt_ready")

    def vector(dve, own):
        own.settle()
        for t in range(TILES):
            own(nc.vector.bn_stats(c.stats[:, t, :], c.X[:, t, :]))
        own.settle()
        for t in range(TILES):
            nc.vector.bn_aggr(c.moments[:, t, :], c.stats[:, t, :]).then_inc(var_ready, 1)
        dve.wait_ge(rstd_ready, k + 1)
        for t in range(TILES):
            nc.vector.tensor_scalar(c.XN[:, t, :], c.X[:, t, :], c.moments[:, t, 0:1], c.rstd[:, t:t + 1],
                                    ALU.subtract, ALU.mult).then_inc(xn_ready, 1)

    def gpsimd(pool, own):
        pool.wait_ge(var_ready, TILES * (k + 1))
        own(nc.gpsimd.tensor_scalar(c.var_eps[:, 0:TILES], c.moments[:, :, 1], 1e-5, None, ALU.add))
        own.settle()
        nc.gpsimd.tensor_tensor(c.rstd[:, 0:TILES], c.var_eps[:, 0:TILES], c.neghalf[:, 0:TILES], ALU.pow).then_inc(rstd_ready, 1)

    def tensor(pe, own):
        for t in range(TILES):
            pe.wait_ge(xn_ready, TILES * k + t + 1)
            nc.tensor.transpose(c.PS[:, t // 4, (t % 4) * 128:(t % 4 + 1) * 128], c.XN[:, t, :], c.ident).then_inc(xt_psum, 1)

    def scalar(act, own):
        for half in range(HALVES):
            act.wait_ge(xt_psum, TILES * k + 4 * half + 4)
            nc.scalar.copy(c.XT[:, 512 * half:512 * half + 512], c.PS[:, half, :]).then_inc(xt_ready, 1)

    return dict(vector=vector, gpsimd=gpsimd, tensor=tensor, scalar=scalar)


def add_output(c, name):
    out_psum = c.sem(name + "_out_psum")

    def vector(dve, own):
        for half in range(HALVES):
            dve.wait_ge(out_psum, half + 1)
            tiles = c.X[:, 4 * half:4 * half + 4, :]
            own(c.nc.vector.tensor_tensor(tiles, c.PS[:, 6 + half, :].rearrange("p (t d) -> p t d", d=D), tiles, ALU.add))
    return vector


def l0_attn(c, k):
    nc, W, PS = c.nc, c.W["l0_attn"], c.PS
    s = c.space
    QR = s(2048).rearrange("p (g t) -> p g t", g=2)
    KR = s(2048).rearrange("p (g t) -> p g t", g=2)
    tmp = s(4 * 1024).rearrange("p (i j t) -> p i j t", i=2, j=4)
    VF = s(1024 + 16)
    V = VF[:, 0:1024].rearrange("p (t d) -> p t d", t=TILES)
    G = s(1024)
    S = s(3 * 768).rearrange("p (r i n) -> p r i n", r=3, i=2)
    Y = s(1024)
    SQ, YT, Z = s(1024), s(1024), s(1024)
    YU = s(1024).rearrange("p (r t) -> p r t", r=2)
    y_copied, y_back, v_pad = c.sem("l0_y_copied"), c.sem("l0_y_back"), c.sem("l0_v_pad")
    mean, var, rstd = s(64), s(64), s(64)
    qk_psum, products, rotated = c.sem("l0_qk_psum"), c.sem("l0_products"), c.sem("l0_rotated")
    v_psum, v_ready, g_psum, g_ready = c.sem("l0_v_psum"), c.sem("l0_v_ready"), c.sem("l0_g_psum"), c.sem("l0_g_ready")
    s_psum, masked, y_psum, y_ready = c.sem("l0_s_psum"), c.sem("l0_masked"), c.sem("l0_y_psum"), c.sem("l0_y_ready")
    y_done, gn_var, gn_rstd, yn_ready = c.sem("l0_y_done"), c.sem("l0_gn_var"), c.sem("l0_gn_rstd"), c.sem("l0_yn_ready")
    yt_psum, yt_ready, gated = c.sem("l0_yt_psum"), c.sem("l0_yt_ready"), c.sem("l0_gated")
    out_psum = c.sem("l0_attn_out_psum")
    PAIRS = 16

    def tensor(pe, own):
        pe.wait_ge(c.loaded["l0_attn"], 16)
        pe.wait_ge(c.sem("xt_ready"), 2 * k + 2)
        for u in range(4):
            g, half = u // 2, u % 2
            if u >= 2:
                pe.wait_ge(products, 4 * (u - 1))
            for i, w in enumerate(("wq", "wqs", "wk", "wks")):
                last = nc.tensor.matmul(PS[:, 4 * (u % 2) + i, :], W[w][:, g * 128:g * 128 + 128],
                                        c.XT[:, 512 * half:512 * half + 512], start=True, stop=True)
            last.then_inc(qk_psum, 1)
        pe.wait_ge(products, 12)
        for t in range(TILES):
            nc.tensor.matmul(PS[:, t // 4, (t % 4) * 128:(t % 4 + 1) * 128], c.XT[:, 128 * t:128 * t + 128], W["wv"],
                             start=True, stop=True).then_inc(v_psum, 1)
        for half in range(HALVES):
            nc.tensor.matmul(PS[:, 2 + half, :], W["wg"], c.XT[:, 512 * half:512 * half + 512],
                             start=True, stop=True).then_inc(g_psum, 1)
        pe.wait_ge(rotated, 8)
        pe.wait_ge(products, 16)

        def scores(p):
            b, hp = p // 4, p % 4
            if p >= 2:
                pe.wait_ge(masked, p - 1)
            for i in range(2):
                h = 2 * hp + i
                g, r = h // 4, 32 * (h % 4)
                bank = PS[:, 4 + 2 * (p % 2) + i, :]
                q, kk = QR[r:r + 32, g, 256 * b:256 * b + 256], KR[r:r + 32, g, 256 * b:256 * b + 256]
                nc.tensor.matmul(bank[:, 0:256], kk[:, 0:128], q, start=True, stop=True)
                last = nc.tensor.matmul(bank[:, 256:384], kk[:, 128:256], q[:, 128:256], start=True, stop=True)
            last.then_inc(s_psum, 1)

        def values(p):
            b, hp = p // 4, p % 4
            if p == 0:
                pe.wait_ge(v_ready, 2)
                pe.wait_ge(v_pad, 1)
            if hp == 0 and b >= 2:
                pe.wait_ge(y_copied, b - 1)
            pe.wait_ge(masked, p + 1)
            for i in range(2):
                h = 2 * hp + i
                sc, row = S[:, p % 3, i, :], 32 * (h % 4)
                v = [VF[:, 128 * (2 * b + kc) + 16 * h:128 * (2 * b + kc) + 16 * h + 32] for kc in range(2)]
                out = PS[row:row + 32, b % 2, 256 * (h // 4):256 * (h // 4) + 256]
                nc.tensor.matmul(out, v[0], sc[:, 0:256], start=True, stop=False, tile_position=(0, row))
                last = nc.tensor.matmul(out[:, 128:256], v[1], sc[:, 256:384], start=False, stop=True, tile_position=(0, row))
            last.then_inc(y_psum, 1)

        def transposed_back(b):
            pe.wait_ge(y_copied, b + 1)
            if b == 0:
                pe.wait_ge(g_ready, 2)
            if b >= 2:
                pe.wait_ge(y_ready, b - 1)
            for qc in range(2):
                for g in range(2):
                    last = nc.tensor.transpose(PS[:, 2 + b % 2, 256 * qc + 128 * g:256 * qc + 128 * g + 128],
                                               YU[:, b % 2, 256 * g + 128 * qc:256 * g + 128 * qc + 128], c.ident)
            last.then_inc(y_back, 1)

        scores(0)
        for p in range(PAIRS):
            if p + 1 < PAIRS:
                scores(p + 1)
            values(p)
            if p >= 5 and p % 4 == 1:
                transposed_back(p // 4 - 1)
        transposed_back(B - 1)
        for t in range(TILES):
            if t == 0:
                pe.wait_ge(y_ready, B)
            pe.wait_ge(yn_ready, t // 2 + 1)
            nc.tensor.transpose(PS[:, 2 + t // 4, (t % 4) * 128:(t % 4 + 1) * 128], Y[:, 128 * t:128 * t + 128], c.ident).then_inc(yt_psum, 1)
        for t in range(TILES):
            pe.wait_ge(gated, t // 4 + 1)
            last = nc.tensor.matmul(PS[:, 6 + t // 4, (t % 4) * 128:(t % 4 + 1) * 128], Z[:, 128 * t:128 * t + 128],
                                    W["wo"], start=True, stop=True)
            if t % 4 == 3:
                last.then_inc(out_psum, 1)

    def vector(dve, own):
        dve.wait_ge(c.consts_loaded, 16)
        for u in range(4):
            g, half = u // 2, u % 2
            dve.wait_ge(qk_psum, u + 1)
            if u >= 2:
                dve.wait_ge(rotated, 2 * (u - 1))
            for i, name in enumerate(("cq", "sq", "ck", "sk")):
                table = bcast(c.const[name][:, 256 * g:256 * g + 256], 1, 2)
                nc.vector.tensor_tensor(tmp[:, u % 2, i, :].rearrange("p (b t) -> p b t", b=2),
                                        PS[:, 4 * (u % 2) + i, :].rearrange("p (b t) -> p b t", b=2),
                                        table, ALU.mult).then_inc(products, 1)
        def centre(b):
            cols = slice(16 * b, 16 * b + 16)
            y3, sq3 = (a[:, 256 * b:256 * b + 256].rearrange("p (n e) -> p n e", e=16) for a in (Y, SQ))
            dve.wait_ge(y_ready, b + 1)
            own(nc.vector.tensor_reduce(mean[:, cols], y3, AX_X, ALU.add))
            own.settle()
            own(nc.vector.tensor_scalar(mean[:, cols], mean[:, cols], 1.0 / 16, None, ALU.mult))
            own.settle()
            own(nc.vector.tensor_tensor(y3, y3, bcast(mean[:, cols], 2, 16), ALU.subtract))
            own.settle()
            own(nc.vector.tensor_tensor(sq3, y3, y3, ALU.mult))
            own.settle()
            nc.vector.tensor_reduce(var[:, cols], sq3, AX_X, ALU.add).then_inc(gn_var, 1)

        def divide(b):
            y3 = Y[:, 256 * b:256 * b + 256].rearrange("p (n e) -> p n e", e=16)
            dve.wait_ge(gn_rstd, b + 1)
            nc.vector.tensor_tensor(y3, y3, bcast(rstd[:, 16 * b:16 * b + 16], 2, 16), ALU.mult).then_inc(yn_ready, 1)

        for p in range(PAIRS):
            if p % 4 == 3 and p >= 7:
                centre(p // 4 - 1)
            if p % 4 == 1 and p >= 9:
                divide(p // 4 - 2)
            dve.wait_ge(s_psum, p + 1)
            if p >= 3:
                dve.wait_ge(y_psum, p - 2)
            b0 = 4 + 2 * (p % 2)
            nc.vector.tensor_tensor(S[:, p % 3, :, :], PS[:, b0:b0 + 2, 0:384], bcast(c.const["tri3"], 1, 2),
                                    ALU.mult).then_inc(masked, 1)
        centre(B - 1)
        divide(B - 2)
        divide(B - 1)
        for half in range(HALVES):
            dve.wait_ge(yt_ready, half + 1)
            dve.wait_ge(g_ready, 2)
            sl = slice(512 * half, 512 * half + 512)
            nc.vector.tensor_tensor(Z[:, sl], YT[:, sl], G[:, sl], ALU.mult).then_inc(gated, 1)
        c.add("l0_attn")(dve, own)

    def gpsimd(pool, own):
        nc.gpsimd.memset(VF[:, 1024:], 0.0).then_inc(v_pad, 1)
        for u in range(4):
            g, half = u // 2, u % 2
            for i, dst in enumerate((QR, KR)):
                pool.wait_ge(products, 4 * u + 2 * i + 2)
                nc.gpsimd.tensor_tensor(dst[:, g, 512 * half:512 * half + 512], tmp[:, u % 2, 2 * i, :],
                                        tmp[:, u % 2, 2 * i + 1, :], ALU.add).then_inc(rotated, 1)
        for b in range(B):
            cols = slice(16 * b, 16 * b + 16)
            pool.wait_ge(gn_var, b + 1)
            own(nc.gpsimd.tensor_scalar(var[:, cols], var[:, cols], 1.0 / 16, 1e-5, ALU.mult, ALU.add))
            own.settle()
            nc.gpsimd.tensor_tensor(rstd[:, cols], var[:, cols], c.neghalf[:, cols], ALU.pow).then_inc(gn_rstd, 1)

    def scalar(act, own):
        for half in range(HALVES):
            act.wait_ge(v_psum, 4 * half + 4)
            nc.scalar.copy(V[:, 4 * half:4 * half + 4, :], PS[:, half, :].rearrange("p (t d) -> p t d", d=D)).then_inc(v_ready, 1)
        for half in range(HALVES):
            act.wait_ge(g_psum, half + 1)
            nc.scalar.activation(G[:, 512 * half:512 * half + 512], PS[:, 2 + half, :], ACT.Silu).then_inc(g_ready, 1)
        for b in range(B):
            act.wait_ge(y_psum, 4 * b + 4)
            if b >= 2:
                act.wait_ge(y_back, b - 1)
            nc.scalar.copy(YU[:, b % 2, :], PS[:, b % 2, :]).then_inc(y_copied, 1)
            act.wait_ge(y_back, b + 1)
            nc.scalar.copy(Y[:, 256 * b:256 * b + 256].rearrange("p (n e) -> p n e", e=16),
                           PS[:, 2 + b % 2, :].rearrange("p (n e) -> p n e", e=32)[:, :, 0:16]).then_inc(y_ready, 1)
        for half in range(HALVES):
            act.wait_ge(yt_psum, 4 * half + 4)
            nc.scalar.activation(YT[:, 512 * half:512 * half + 512], PS[:, 2 + half, :], ACT.Identity,
                                 bias=W["gnb"], scale=W["gnw"]).then_inc(yt_ready, 1)

    return dict(tensor=tensor, vector=vector, gpsimd=gpsimd, scalar=scalar)


HEADS = 16
UNITS = B * HEADS
LAG = HEADS + 8


def attention(c, n, *, max_scores, exp_scores, values, place_max, dv, heads_a_bank, normed, causal=False,
              start=None, start_batch=None, extra=None, P=None, work=None, head_order=lambda h: h,
              lag=LAG, steps=UNITS + LAG, transposed=None):
    nc, PS = c.nc, c.PS
    MX, MR, MP, MT, RD = work
    qk1, max_done, max_parts = c.sem(n + "_scores1_psum"), c.sem(n + "_max_done"), c.sem(n + "_max_parts")
    mt_psum, mt_ready, max_placed = c.sem(n + "_maxT_psum"), c.sem(n + "_maxT_ready"), c.sem(n + "_max_placed")
    qk2, exp_done, pv_done, norm_done = c.sem(n + "_scores2_psum"), c.sem(n + "_exp_done"), c.sem(n + "_pv_done"), c.sem(n + "_norm_done")
    RING = P.shape[1]
    KEYS = 384 if causal else 512
    NV = UNITS // heads_a_bank
    if transposed is not None:
        copied, back = c.sem(n + "_outT_copied"), c.sem(n + "_out_back")
        after = lambda v: lag + 8 * v + 11
        uses = sorted([(HEADS * (b + 1) + 2, "max", b) for b in range(B)] + [(after(v), "out", v) for v in range(UNITS // 8)])
        steps = after(UNITS // 8 - 1) + 1

    def tensor(pe, own):
        if start is not None:
            start(pe)

        def first(a):
            if start_batch is not None and a % HEADS == 0:
                start_batch(pe, a // HEADS)
            if a >= 3:
                pe.wait_ge(max_done, a - 2)
            max_scores(a // HEADS, a % HEADS, PS[:, a % 3, :]).then_inc(qk1, 1)

        def transposed_max(b):
            pe.wait_ge(max_parts, b + 1)
            if transposed is not None:
                bank7_is_free((HEADS * (b + 1) + 2, "max", b))
            elif b >= 1:
                pe.wait_ge(mt_ready, b)
            for qc in range(2):
                last = nc.tensor.transpose(PS[0:48, 7, 64 * qc:64 * qc + 64].bitcast(BF16), MP[:, b % 2, qc, :], c.identb)
            last.then_inc(mt_psum, 1)

        def second(i):
            if i % HEADS == 0:
                pe.wait_ge(max_placed, 16 * place_max.dmas * (i // HEADS + 1))
            if i >= 2:
                pe.wait_ge(exp_done, i - 1)
            exp_scores(i // HEADS, i % HEADS, PS[:, 3 + i % 2, :]).then_inc(qk2, 1)

        def bank7_is_free(use):
            before = [u for u in uses if u < use]
            if before and before[-1][1] == "max":
                pe.wait_ge(mt_ready, before[-1][2] + 1)
            elif before:
                pe.wait_ge(norm_done, before[-1][2] + 1)

        def weighted_transposed(i):
            b, h, v = i // HEADS, i % HEADS, i // 8
            if i % 8 == 0 and v >= 2:
                pe.wait_ge(copied, v - 1)
            pe.wait_ge(exp_done, i + 1)
            p, row, col = P[:, i % RING, :], 32 * (h % 4), 256 * (h // 4 % 2)
            out = PS[row:row + 32, 5 + v % 2, col:col + 256]
            nc.tensor.matmul(out, values(b, 0, h), p[:, 0:256], start=True, stop=False, tile_position=(0, row))
            if causal:
                last = nc.tensor.matmul(out[:, 128:256], values(b, 1, h), p[:, 256:384], start=False, stop=True, tile_position=(0, row))
            else:
                last = nc.tensor.matmul(out, values(b, 1, h), p[:, 256:512], start=False, stop=True, tile_position=(0, row))
            last.then_inc(pv_done, 1)

        def transposed_back(v):
            pe.wait_ge(copied, v + 1)
            bank7_is_free((after(v), "out", v))
            for qc in range(2):
                for g in range(2):
                    last = nc.tensor.transpose(PS[:, 7, 256 * qc + 128 * g:256 * qc + 128 * g + 128],
                                               transposed[:, v % 2, 256 * g + 128 * qc:256 * g + 128 * qc + 128], c.ident)
            last.then_inc(back, 1)

        def weighted(i):
            if transposed is not None:
                return weighted_transposed(i)
            b, h, v = i // HEADS, i % HEADS, i // heads_a_bank
            if i % heads_a_bank == 0 and v >= 2:
                pe.wait_ge(norm_done, v - 1)
            pe.wait_ge(exp_done, i + 1)
            p = P[:, i % RING, :]
            for qc in range(2):
                at = (qc * heads_a_bank + h % heads_a_bank) * (dv + 1)
                out = PS[:, 5 + v % 2, at:at + dv + 1]
                if causal:
                    steps = [(0, 0)] if qc == 0 else [(0, 128), (1, 256)]
                else:
                    steps = [(kc, 256 * kc + 128 * qc) for kc in range(2)]
                for j, (kc, col) in enumerate(steps):
                    last = nc.tensor.matmul(out, p[:, col:col + 128], values(b, kc, h), start=j == 0, stop=j == len(steps) - 1)
            last.then_inc(pv_done, 1)

        for step in range(steps):
            if extra is not None:
                extra["tensor"](pe, step)
            if step >= HEADS + 2 and (step - 2) % HEADS == 0 and step // HEADS <= B:
                if extra is not None:
                    extra["before_max"](pe, step)
                transposed_max(step // HEADS - 1)
            if step < UNITS:
                first(step)
            i = step - lag
            if 0 <= i < UNITS:
                second(i)
            if 1 <= i <= UNITS:
                weighted(i - 1)
            if transposed is not None and i >= 11 and (i - 11) % 8 == 0:
                transposed_back((i - 11) // 8)
        if steps <= UNITS + lag:
            weighted(UNITS - 1)

    def scalar(act, own):
        for step in range(steps):
            if extra is not None:
                extra["scalar"](act, step)
            if step >= HEADS + 2 and (step - 2) % HEADS == 0 and step // HEADS <= B:
                b = step // HEADS - 1
                act.wait_ge(mt_psum, b + 1)
                if b >= 1:
                    act.wait_ge(max_placed, 16 * place_max.dmas * b)
                nc.scalar.copy(MT, PS[0:48, 7, 0:128].bitcast(BF16)).then_inc(mt_ready, 1)
            i = step - lag
            if transposed is not None and i >= 9 and (i - 9) % 8 == 0 and (i - 9) // 8 < UNITS // 8:
                v = (i - 9) // 8
                act.wait_ge(pv_done, 8 * (v + 1))
                if v >= 2:
                    act.wait_ge(back, v - 1)
                nc.scalar.copy(transposed[:, v % 2, :], PS[:, 5 + v % 2, :]).then_inc(copied, 1)
            if 0 <= i < UNITS:
                act.wait_ge(qk2, i + 1)
                if i >= RING:
                    act.wait_ge(pv_done, i - RING + 1)
                nc.scalar.activation(P[:, i % RING, 0:KEYS], PS[:, 3 + i % 2, 0:KEYS], ACT.Exp).then_inc(exp_done, 1)

    def vector(dve, own):
        def maxima(a):
            b, h = a // HEADS, head_order(a % HEADS)
            dve.wait_ge(qk1, a + 1)
            if causal:
                own(nc.vector.tensor_reduce(MX[:, b % 2, 0, h:h + 1], PS[:, a % 3, 0:128], AX_X, ALU.max))
                nc.vector.tensor_reduce(MX[:, b % 2, 1, h:h + 1], PS[:, a % 3, 128:384], AX_X, ALU.max).then_inc(max_done, 1)
            else:
                nc.vector.tensor_reduce(MX[:, b % 2, :, h], PS[:, a % 3, :].rearrange("p (c k) -> p c k", c=2),
                                        AX_X, ALU.max).then_inc(max_done, 1)
            if a % HEADS == HEADS - 1:
                dve.wait_ge(max_done, a + 1)
                own.settle()
                m = MX[:, b % 2, :, :]
                part = [MP[:, b % 2, :, 16 * i:16 * i + 16] for i in range(3)]
                own(nc.vector.tensor_scalar(part[0], m, -1.0, None, ALU.mult))
                own.settle()
                own(nc.vector.scalar_tensor_tensor(MR, m, -1.0, part[0], ALU.mult, ALU.subtract))
                own.settle()
                own(nc.vector.tensor_copy(part[1], MR))
                own.settle()
                nc.vector.tensor_tensor(part[2], MR, part[1], ALU.subtract).then_inc(max_parts, 1)

        def normalise(v):
            i = v * heads_a_bank
            dve.wait_ge(pv_done, i + heads_a_bank)
            o = PS[:, 5 + v % 2, 0:2 * heads_a_bank * (dv + 1)].rearrange("p (c h d) -> p c h d", c=2, d=dv + 1)
            own(nc.vector.reciprocal(RD[:, v % 2, :, :], o[:, :, :, dv]))
            own.settle()
            nc.vector.tensor_tensor(normed(i // HEADS, i % HEADS), o[:, :, :, 0:dv],
                                    bcast(RD[:, v % 2, :, :], 3, dv), ALU.mult).then_inc(norm_done, 1)

        def normalise_back(v):
            dve.wait_ge(back, v + 1)
            o = PS[:, 7, :].rearrange("p (c h e) -> p c h e", c=2, e=32)
            own(nc.vector.reciprocal(RD[:, v % 2, :, :], o[:, :, :, dv]))
            own.settle()
            nc.vector.tensor_tensor(normed(v // 2, 8 * (v % 2)), o[:, :, :, 0:dv],
                                    bcast(RD[:, v % 2, :, :], 3, dv), ALU.mult).then_inc(norm_done, 1)

        for step in range(steps + 3):
            if extra is not None and "vector" in extra:
                extra["vector"](dve, own, step)
            if step < UNITS:
                maxima(step)
            i = step - lag - 2
            if transposed is not None:
                i = step - lag - 12
                if i >= 0 and i % 8 == 0 and i // 8 < UNITS // 8:
                    normalise_back(i // 8)
            elif 0 <= i < UNITS and i % heads_a_bank == heads_a_bank - 1:
                normalise(i // heads_a_bank)

    def sync(sp, own):
        for b in range(B):
            sp.wait_ge(mt_ready, b + 1)
            place_max(sp, b, max_placed)

    return dict(tensor=tensor, scalar=scalar, vector=vector, sync=sync), NV


def attention_work(c, heads_a_bank, ring=4):
    s = c.space
    MX = s(2 * 32).rearrange("p (r c h) -> p r c h", r=2, c=2)
    MR = s(32).rearrange("p (c h) -> p c h", c=2)
    MP = s(2 * 96, BF16).rearrange("p (r c m) -> p r c m", r=2, c=2)
    MT = s(256, BF16)[0:48, :]
    RD = s(2 * 2 * heads_a_bank).rearrange("p (r c h) -> p r c h", r=2, c=2)
    P = s(ring * 512).rearrange("p (r k) -> p r k", r=ring) if ring else None
    return (MX, MR, MP, MT, RD), P


def split_parts(engine, own, parts, rest, full):
    own(engine.tensor_copy(parts[:, 0, :], full))
    own.settle()
    own(engine.tensor_tensor(rest, full, parts[:, 0, :], ALU.subtract))
    own.settle()
    own(engine.tensor_copy(parts[:, 1, :], rest))
    own.settle()
    return engine.tensor_tensor(parts[:, 2, :], rest, parts[:, 1, :], ALU.subtract)


Q_RUNS = ((0, 3, 0), (3, 2, 1), (5, 1, 2))
K_RUNS = ((0, 3, 0), (3, 2, 0), (5, 1, 0))


def stacked_attention(c, k, name, kind):
    nc, W, PS, s = c.nc, c.W[name], c.PS, c.space
    mqa, causal = kind == "mqa", kind == "causal"
    SCALE = 8 ** -0.5
    MROW = 54 if causal else 48
    QZ = s(8 * TOKENS // 2)
    QS = QZ.bitcast(BF16).rearrange("p (f g t) -> p f g t", f=2, g=8)
    KG = 1 if mqa else 8
    KZ = s(KG * TOKENS)
    KS = KZ.bitcast(BF16).rearrange("p (f r g t) -> p f r g t", f=2, r=2, g=KG)
    QF, KF = s(TOKENS), s(TOKENS)
    shared = s(3 * TOKENS)
    QP, KP = (shared[:, 1536 * i:1536 * i + 1536].bitcast(BF16).rearrange("p (i t) -> p i t", i=3) for i in range(2))
    P = shared[:, 0:2048].rearrange("p (r k) -> p r k", r=4)
    OU = shared[:, 2048:3072].rearrange("p (r t) -> p r t", r=2)
    rest_q, rest_k = s(TOKENS), s(TOKENS)
    ON = rest_k.rearrange("p (t d) -> p t d", t=TILES)
    VH = 1 if mqa else 16
    VAF = s(TILES * VH * 9 + 24)
    VA = VAF[:, 0:TILES * VH * 9].rearrange("p (t h e) -> p t h e", t=TILES, h=VH)
    OT = rest_q
    work, _ = attention_work(c, 8, ring=0)
    KR = 8 if mqa else 128
    scratch_q = c.nc.dram_tensor(name + "_scratch_q", [2, 3, 128, 512], BF16, kind="Internal").ap()
    scratch_k = c.nc.dram_tensor(name + "_scratch_k", [2, 3, KR, 512], BF16, kind="Internal").ap()
    q_psum, k_psum, v_psum = (c.sem(name + x) for x in ("_q_psum", "_k_psum", "_v_psum"))
    q_full, k_full, v_ready, v_ones = (c.sem(name + x) for x in ("_q_full", "_k_full", "_v_ready", "_v_ones"))
    q_parts, k_parts = c.sem(name + "_q_parts"), c.sem(name + "_k_parts")
    q_saved, k_saved = c.sem(name + "_q_saved"), c.sem(name + "_k_saved")
    q_stacked, k_stacked = ([c.sem(name + x + str(half)) for half in range(HALVES)] for x in ("_q_stacked", "_k_stacked"))
    ot_psum, ot_ready, out_psum = c.sem(name + "_ot_psum"), c.sem(name + "_ot_ready"), c.sem(name + "_out_psum")
    src = c.XT if causal else c.CTXT
    CONSTANTS = 4 if causal else 2
    A_HALF = 2 * len(Q_RUNS)
    zeroed, constant = c.sem(name + "_zeroed"), c.sem(name + "_constant")

    def rows(b, h):
        f, at = b // 2, 256 * (b % 2)
        return QS[:, f, h // 2, at:at + 256], KS[:, f, h % 2, 0 if mqa else h // 2, at:at + 256]

    def max_scores(b, h, bank):
        q, kk = rows(b, h)
        if causal:
            nc.tensor.matmul(bank[:, 0:128], q[:, 0:128], kk[:, 0:128], start=True, stop=False)
            nc.tensor.matmul(bank[:, 0:128], c.identb, c.mask_qk, start=False, stop=True)
            nc.tensor.matmul(bank[:, 128:256], q[:, 128:256], kk[:, 0:128], start=True, stop=True)
            nc.tensor.matmul(bank[:, 256:384], q[:, 128:256], kk[:, 128:256], start=True, stop=False)
            return nc.tensor.matmul(bank[:, 256:384], c.identb, c.mask_qk, start=False, stop=True)
        nc.tensor.matmul(bank[:, 0:256], q[:, 0:128], kk, start=True, stop=True)
        return nc.tensor.matmul(bank[:, 256:512], q[:, 128:256], kk, start=True, stop=True)

    def exp_scores(b, h, bank):
        q, kk = rows(b, h)
        if causal:
            nc.tensor.matmul(bank[:, 128:256], kk[:, 0:128], q[:, 128:256], start=True, stop=True)
            nc.tensor.matmul(bank[:, 0:128], kk[:, 0:128], q[:, 0:128], start=True, stop=False)
            nc.tensor.matmul(bank[:, 0:128], c.identb, c.mask_kq, start=False, stop=True)
            nc.tensor.matmul(bank[:, 256:384], kk[:, 128:256], q[:, 128:256], start=True, stop=False)
            return nc.tensor.matmul(bank[:, 256:384], c.identb, c.mask_kq, start=False, stop=True)
        nc.tensor.matmul(bank[:, 0:256], kk[:, 0:128], q, start=True, stop=True)
        return nc.tensor.matmul(bank[:, 256:512], kk[:, 128:256], q, start=True, stop=True)

    def values(b, kc, h):
        at = 9 * ((2 * b + kc) * VH + (0 if mqa else h))
        return VAF[:, at:at + 32]

    def place_max(sp, b, placed):
        if b == 0:
            sp.wait_ge(k_saved, 16 * HALVES)
        for part in range(3):
            for r in range(2):
                row, at = 64 * r + MROW + part, 256 * (b % 2)
                sp.dma_start(QS[row:row + 1, b // 2, :, at:at + 256],
                             work[3][16 * part + 8 * r:16 * part + 8 * r + 8, :]).then_inc(placed, 16)
    place_max.dmas = 6

    def start_batch(pe, b):
        if b % 2 == 0:
            pe.wait_ge(q_stacked[b // 2], 16 * A_HALF)
            pe.wait_ge(k_stacked[b // 2], 16 * A_HALF)
            pe.wait_ge(constant, 16 * CONSTANTS)
        if b == 0:
            pe.wait_ge(v_ready, 2)
            pe.wait_ge(v_ones, 2)

    main, NV = attention(c, name, max_scores=max_scores, exp_scores=exp_scores,
                         values=values, place_max=place_max, dv=8, transposed=OU,
                         heads_a_bank=8, causal=causal, start_batch=start_batch, P=P, work=work, head_order=lambda h: (h % 2) * 8 + h // 2,
                         normed=lambda b, h: ON[:, 2 * b:2 * b + 2, 8 * h:8 * h + 64].rearrange("p c (h d) -> p c h d", d=8))

    def tensor(pe, own):
        pe.wait_ge(c.loaded[name], 16)
        for half in range(HALVES):
            if half == 0 and causal:
                pe.wait_ge(c.sem("xt_ready"), 2 * k + 2)
            nc.tensor.matmul(PS[0:KR, 4 + half, :], W["wk"], src[:, 512 * half:512 * half + 512], start=True, stop=True).then_inc(k_psum, 1)
        pe.wait_ge(c.sem("xt_ready"), 2 * k + 2)
        for half in range(HALVES):
            nc.tensor.matmul(PS[:, 2 + half, :], W["wq"], c.XT[:, 512 * half:512 * half + 512], start=True, stop=True).then_inc(q_psum, 1)
        VC = 8 if mqa else 128
        for t in range(TILES):
            out = PS[:, 6 + t // 4, (t % 4) * VC:(t % 4 + 1) * VC]
            last = nc.tensor.matmul(out, src[:, 128 * t:128 * t + 128], W["wv"], start=True, stop=mqa)
            if not mqa:
                last = nc.tensor.matmul(out, c.ones_row[0:1, :], W["bv"], start=False, stop=True)
            if t % 4 == 3:
                last.then_inc(v_psum, 1)
        main["tensor"](pe, own)
        pe.wait_ge(c.sem(name + "_exp_done"), UNITS)
        for t in range(TILES):
            if t % 2 == 0:
                pe.wait_ge(c.sem(name + "_norm_done"), t + 2)
            nc.tensor.transpose(PS[:, t // 4, (t % 4) * 128:(t % 4 + 1) * 128], ON[:, t, :], c.ident).then_inc(ot_psum, 1)
        for t in range(TILES):
            pe.wait_ge(ot_ready, t // 4 + 1)
            out = PS[:, 6 + t // 4, (t % 4) * 128:(t % 4 + 1) * 128]
            last = nc.tensor.matmul(out, OT[:, 128 * t:128 * t + 128], W["wo"], start=True, stop=mqa)
            if not mqa:
                last = nc.tensor.matmul(out, c.ones_row[0:1, :], W["bo"], start=False, stop=True)
            if t % 4 == 3:
                last.then_inc(out_psum, 1)

    def scalar(act, own):
        for half in range(HALVES):
            act.wait_ge(k_psum, half + 1)
            dst, ps = KF[0:KR, 512 * half:512 * half + 512], PS[0:KR, 4 + half, :]
            if mqa:
                nc.scalar.copy(dst, ps).then_inc(k_full, 1)
            else:
                nc.scalar.activation(dst, ps, ACT.Identity, bias=W["bk"]).then_inc(k_full, 1)
        for half in range(HALVES):
            act.wait_ge(v_psum, half + 1)
            if half == 0:
                act.wait_ge(v_ones, 2)
            VC = 8 if mqa else 128
            nc.scalar.copy(VA[:, 4 * half:4 * half + 4, :, 0:8],
                           PS[:, 6 + half, 0:4 * VC].rearrange("p (t h e) -> p t h e", t=4, e=8)).then_inc(v_ready, 1)
        for half in range(HALVES):
            cols = slice(512 * half, 512 * half + 512)
            act.wait_ge(k_parts, half + 1)
            act.dma_start(scratch_k[half].rearrange("i p t -> p i t"), KP[0:KR, :, cols]).then_inc(k_saved, 16)
            act.wait_ge(k_saved, 16 * (half + 1))
            for r in range(2):
                for slot, n, part in K_RUNS:
                    src_rows = scratch_k[half, part:part + n, 0 if mqa else 64 * r:8 if mqa else 64 * r + 64, :]
                    src_rows = src_rows.rearrange("i (e g) t -> i e (g t)", e=8)
                    dst = KS[64 * r + 8 * slot:64 * r + 8 * (slot + n), half, r].rearrange("p g t -> p (g t)")
                    act.dma_start(dst, src_rows).then_inc(k_stacked[half], 16)
        main["scalar"](act, own)
        for half in range(HALVES):
            act.wait_ge(ot_psum, 4 * half + 4)
            nc.scalar.copy(OT[:, 512 * half:512 * half + 512], PS[:, half, :]).then_inc(ot_ready, 1)

    def vector(dve, own):
        nc.vector.memset(QZ, 0.0).then_inc(zeroed, 1)
        for half in range(HALVES):
            dve.wait_ge(q_psum, half + 1)
            if mqa:
                own(nc.vector.tensor_scalar(QF[:, 512 * half:512 * half + 512], PS[:, 2 + half, :], SCALE, None, ALU.mult))
            else:
                own(nc.vector.tensor_scalar(QF[:, 512 * half:512 * half + 512], PS[:, 2 + half, :], W["bq"], SCALE, ALU.add, ALU.mult))
        own.settle()
        for half in range(HALVES):
            cols = slice(512 * half, 512 * half + 512)
            split_parts(nc.vector, own, QP[:, :, cols], rest_q[:, cols], QF[:, cols]).then_inc(q_parts, 1)
        main["vector"](dve, own)
        c.add(name)(dve, own)

    def gpsimd(pool, own):
        pool.wait_ge(c.sem("ln_var_ready"), TILES * (k + 1))
        nc.gpsimd.memset(KZ, 0.0).then_inc(zeroed, 1)
        for half in range(HALVES):
            cols = slice(512 * half, 512 * half + 512)
            pool.wait_ge(k_full, half + 1)
            split_parts(nc.gpsimd, own, KP[0:KR, :, cols], rest_k[0:KR, cols], KF[0:KR, cols]).then_inc(k_parts, 1)
        nc.gpsimd.memset(VAF[:, TILES * VH * 9:], 0.0).then_inc(v_ones, 1)
        nc.gpsimd.memset(VA[:, :, :, 8:9], 1.0).then_inc(v_ones, 1)

    def sync(sp, own):
        sk, sq = c.ins["stack_k"].bitcast(BF16), c.ins["stack_q"].bitcast(BF16)
        sp.wait_ge(zeroed, 2)
        for r in range(2):
            if causal:
                sp.dma_start(KS[64 * r + 48:64 * r + 57, :, r], sk[r]).then_inc(constant, 16)
                sp.dma_start(QS[64 * r + 48:64 * r + 54], sq[r]).then_inc(constant, 16)
            else:
                sp.dma_start(KS[64 * r + 48:64 * r + 51, :, r], sk[r, 3:6, :, 0:KG]).then_inc(constant, 16)
        for half in range(HALVES):
            sp.wait_ge(q_parts, half + 1)
            sp.dma_start(scratch_q[half].rearrange("i p t -> p i t"), QP[:, :, 512 * half:512 * half + 512]).then_inc(q_saved, 16)
            sp.wait_ge(q_saved, 16 * (half + 1))
            for r in range(2):
                for slot, n, part in Q_RUNS:
                    src_rows = bcast(scratch_q[half, part, 64 * r:64 * r + 64, :].rearrange("(e g) t -> e (g t)", e=8), 0, n)
                    dst = QS[64 * r + 8 * slot:64 * r + 8 * (slot + n), half].rearrange("p g t -> p (g t)")
                    sp.dma_start(dst, src_rows).then_inc(q_stacked[half], 16)
        main["sync"](sp, own)

    return dict(tensor=tensor, vector=vector, gpsimd=gpsimd, scalar=scalar, sync=sync)


def l0_xattn(c, k):
    return stacked_attention(c, k, "l0_xattn", "mqa")


def l2_attn(c, k):
    return stacked_attention(c, k, "l2_attn", "causal")


def l2_xattn(c, k):
    return stacked_attention(c, k, "l2_xattn", "full")


def route_parts(c, n, own_engine, own, source, parts):
    nc = c.nc
    rest = c.route_rest[:, 0:parts.shape[1], 0:n]
    part = [parts[:, :, 32 * i:32 * i + n] for i in range(3)]
    own(nc.vector.tensor_copy(part[0], source))
    own.settle()
    own(nc.vector.tensor_tensor(rest, source, part[0], ALU.subtract))
    own.settle()
    own(nc.vector.tensor_copy(part[1], rest))
    own.settle()
    return nc.vector.tensor_tensor(part[2], rest, part[1], ALU.subtract)


def first_maximum(c, own, dst, value, maximum, scratch, iota):
    nc = c.nc
    n, e = value.shape[1], value.shape[2]
    order = bcast(iota, 1, n)
    own(nc.vector.tensor_tensor(scratch, value, bcast(maximum, 2, e), ALU.is_equal))
    own.settle()
    own(nc.vector.tensor_tensor(scratch, scratch, order, ALU.mult))
    own.settle()
    own(nc.vector.tensor_reduce(c.route_max[:, 0:n], scratch, AX_X, ALU.max))
    own.settle()
    own(nc.vector.tensor_tensor(dst, scratch, bcast(c.route_max[:, 0:n], 2, e), ALU.is_equal))
    own.settle()


def gated_experts(c, k, name, experts, units, choose, scale_gate):
    nc, W, PS, s = c.nc, c.W[name], c.PS, c.space
    SX = s(2 * TOKENS).rearrange("p (r t) -> p r t", r=2)
    SG = s(2 * 512).rearrange("p (r t) -> p r t", r=2)
    H = s(2 * TOKENS).rearrange("p (r t) -> p r t", r=2)
    parts = s(TILES * 96, BF16).rearrange("p (t m) -> p t m", t=TILES)
    RT = s(TOKENS, BF16)[0:96, :]
    LG, A1, A2, A3, C = (s(TILES * experts).rearrange("p (t e) -> p t e", t=TILES) for _ in range(5))
    small = [s(TILES) for _ in range(4)]
    logits_psum, logits_read, route_act = c.sem(name + "_logits_psum"), c.sem(name + "_logits_read"), c.sem(name + "_route_act")
    parts_zero, parts_ready, rt_psum, rt_ready = (c.sem(name + x) for x in ("_parts_zero", "_parts_ready", "_rt_psum", "_rt_ready"))
    spread, scaled, gate_psum, silu_done, hidden, down_done = (c.sem(name + x) for x in (
        "_spread", "_scaled", "_gate_psum", "_silu_done", "_hidden", "_down_done"))
    out_psum = c.sem(name + "_out_psum")
    order = [e for i, (e, *_) in enumerate(units) if e is not None and (i == 0 or units[i - 1][0] != e)]
    turn = {e: i for i, e in enumerate(order)}
    NU = len(units)

    def starts(j):
        if j < NU and units[j][0] is not None and units[j - 1][0] != units[j][0]:
            return units[j][0]
        return None

    def tensor(pe, own):
        pe.wait_ge(c.loaded[name], 16)
        pe.wait_ge(c.sem("xt_ready"), 2 * k + 2)
        for t in range(TILES):
            last = nc.tensor.matmul(PS[:, 0, t * experts:(t + 1) * experts], c.XT[:, 128 * t:128 * t + 128], W["router"], start=True, stop=True)
        last.then_inc(logits_psum, 1)

        def transposed_routes():
            pe.wait_ge(parts_ready, 1)
            for t in range(TILES):
                last = nc.tensor.transpose(PS[0:96, 0, 64 * t:64 * t + 64].bitcast(BF16), parts[:, t, :], c.identb)
            last.then_inc(rt_psum, 1)

        def spread_routes(e):
            i = turn[e]
            if i == 0:
                pe.wait_ge(rt_ready, 1)
            else:
                pe.wait_ge(scaled, 2 * i)
            for half in range(HALVES):
                nc.tensor.matmul(PS[:, half, :], c.sel[0:96, e, :], RT[:, 512 * half:512 * half + 512], start=True, stop=True).then_inc(spread, 1)

        def gate_up(j):
            e, gate, up, _ = units[j]
            for half in range(HALVES):
                x = c.XT[:, 512 * half:512 * half + 512]
                sx = x
                if e is not None:
                    pe.wait_ge(scaled, 2 * turn[e] + half + 1)
                    sx = SX[:, turn[e] % 2, 512 * half:512 * half + 512]
                if j >= 1:
                    pe.wait_ge(hidden, 2 * (j - 1) + half + 1)
                nc.tensor.matmul(PS[:, 2 + 2 * half, :], gate, sx if scale_gate else x, start=True, stop=True).then_inc(gate_psum, 1)
                nc.tensor.matmul(PS[:, 3 + 2 * half, :], up, sx, start=True, stop=True).then_inc(gate_psum, 1)

        def down(j):
            for t in range(TILES):
                if t % 4 == 0:
                    pe.wait_ge(hidden, 2 * j + t // 4 + 1)
                last = nc.tensor.matmul(PS[:, 6 + t // 4, (t % 4) * 128:(t % 4 + 1) * 128], H[:, j % 2, 128 * t:128 * t + 128],
                                        units[j][3], start=j == 0 and t % 4 == 0, stop=j == NU - 1, skip_group_check=True)
                if j == NU - 1 and t % 4 == 3:
                    last.then_inc(out_psum, 1)
            if j < NU - 1:
                last.then_inc(down_done, 1)

        for j in range(NU):
            if j == 2:
                transposed_routes()
            e = starts(j + 1)
            if e is not None:
                spread_routes(e)
            gate_up(j)
            if j >= 1:
                down(j - 1)
        down(NU - 1)

    def scalar(act, own):
        for j in range(NU):
            if j == 1:
                choose[1](act, LG, A1, route_act)
            if j == 2:
                act.wait_ge(rt_psum, 1)
                nc.scalar.copy(RT, PS[0:96, 0, :].bitcast(BF16)).then_inc(rt_ready, 1)
            for half in range(HALVES):
                act.wait_ge(gate_psum, 4 * j + 2 * half + 1)
                if j >= 1:
                    act.wait_ge(hidden, 2 * (j - 1) + half + 1)
                nc.scalar.activation(SG[:, half, :], PS[:, 2 + 2 * half, :], ACT.Silu).then_inc(silu_done, 1)

    def vector(dve, own):
        dve.wait_ge(logits_psum, 1)
        nc.vector.tensor_copy(LG, PS[:, 0, 0:TILES * experts].rearrange("p (t e) -> p t e", t=TILES)).then_inc(logits_read, 1)
        dve.wait_ge(logits_read, 1)

        def scale(e):
            i = turn[e]
            for half in range(HALVES):
                dve.wait_ge(spread, 2 * i + half + 1)
                nc.vector.tensor_tensor(SX[:, i % 2, 512 * half:512 * half + 512], PS[:, half, :],
                                        c.XT[:, 512 * half:512 * half + 512], ALU.mult).then_inc(scaled, 1)

        def hide(j):
            for half in range(HALVES):
                dve.wait_ge(silu_done, 2 * j + half + 1)
                dve.wait_ge(gate_psum, 4 * j + 2 * half + 2)
                if j >= 2 and half == 0:
                    dve.wait_ge(down_done, j - 1)
                nc.vector.tensor_tensor(H[:, j % 2, 512 * half:512 * half + 512], PS[:, 3 + 2 * half, :], SG[:, half, :],
                                        ALU.mult).then_inc(hidden, 1)

        def routes():
            choose[0](dve, own, LG, A1, A2, A3, C, small, route_act)
            dve.wait_ge(parts_zero, 1)
            route_parts(c, experts, nc.vector, own, C, parts).then_inc(parts_ready, 1)

        for j in range(NU):
            if j == 1:
                routes()
            e = starts(j + 1)
            if e is not None:
                scale(e)
            hide(j)
        c.add(name)(dve, own)

    def gpsimd(pool, own):
        pool.wait_ge(c.sem("ln_var_ready"), TILES * (k + 1))
        nc.gpsimd.memset(parts, 0.0).then_inc(parts_zero, 1)

    return dict(tensor=tensor, vector=vector, scalar=scalar, gpsimd=gpsimd)


def l0_ffn(c, k):
    nc = c.nc
    W = c.W["l0_ffn"]
    units = [(None, W["s_gate"][:, 128 * i:128 * i + 128], W["s_up"][:, 128 * i:128 * i + 128], W["s_down"][:, 128 * i:128 * i + 128])
             for i in range(4)]
    units += [(e, W["gate_up"][:, 256 * e:256 * e + 128], W["gate_up"][:, 256 * e + 128:256 * e + 256], W["down"][:, 128 * e:128 * e + 128])
              for e in range(16)]

    def choose_act(act, LG, A1, route_act):
        act.wait_ge(c.sem("l0_ffn_logits_read"), 1)
        nc.scalar.activation(A1, LG, ACT.Sigmoid).then_inc(route_act, 1)

    def choose(dve, own, LG, A1, A2, A3, C, small, route_act):
        own(nc.vector.tensor_reduce(small[0], LG, AX_X, ALU.max))
        own.settle()
        first_maximum(c, own, A3, LG, small[0], A2, c.const["iota16"])
        dve.wait_ge(route_act, 1)
        own(nc.vector.tensor_tensor(C, A3, A1, ALU.mult))
        own.settle()

    return gated_experts(c, k, "l0_ffn", 16, units, (choose, choose_act), True)


def l3_ffn(c, k):
    nc = c.nc
    W = c.W["l3_ffn"]
    units = [(None if e == 0 else e - 1,) + tuple(W[n][:, 512 * e + 128 * i:512 * e + 128 * i + 128] for n in ("gate", "up", "down"))
             for e in range(8) for i in range(4)]

    def choose_act(act, LG, A1, route_act):
        act.wait_ge(c.sem("l3_ffn_shifted"), 1)
        nc.scalar.activation(A1, A1, ACT.Exp).then_inc(route_act, 1)

    def choose(dve, own, LG, A1, A2, A3, C, small, route_act):
        top, total, second, inverse = small
        own(nc.vector.tensor_reduce(top, LG, AX_X, ALU.max))
        own.settle()
        nc.vector.tensor_tensor(A1, LG, bcast(top, 2, 7), ALU.subtract).then_inc(c.sem("l3_ffn_shifted"), 1)
        dve.wait_ge(route_act, 1)
        own(nc.vector.tensor_reduce(total, A1, AX_X, ALU.add))
        own.settle()
        own(nc.vector.reciprocal(inverse, total))
        own.settle()
        own(nc.vector.tensor_tensor(A1, A1, bcast(inverse, 2, 7), ALU.mult))
        own.settle()
        own(nc.vector.tensor_reduce(top, A1, AX_X, ALU.max))
        own.settle()
        first_maximum(c, own, C, A1, top, A2, c.const["iota8"][:, 0:7])
        own(nc.vector.scalar_tensor_tensor(LG, C, -2.0, A1, ALU.mult, ALU.add))
        own.settle()
        own(nc.vector.tensor_reduce(second, LG, AX_X, ALU.max))
        own.settle()
        first_maximum(c, own, A3, LG, second, A2, c.const["iota8"][:, 0:7])
        own(nc.vector.tensor_tensor(total, top, second, ALU.add))
        own(nc.vector.tensor_tensor(C, C, A3, ALU.add))
        own.settle()
        own(nc.vector.tensor_scalar(total, total, 1e-9, None, ALU.add))
        own(nc.vector.tensor_tensor(C, C, A1, ALU.mult))
        own.settle()
        own(nc.vector.reciprocal(inverse, total))
        own.settle()
        own(nc.vector.tensor_tensor(C, C, bcast(inverse, 2, 7), ALU.mult))
        own.settle()

    return gated_experts(c, k, "l3_ffn", 7, units, (choose, choose_act), False)


def l1_attn(c, k):
    nc, W, PS, s = c.nc, c.W["l1_attn"], c.PS, c.space
    qk, qks, lam, WO = s(1), s(1), s(1), s(128)
    V, O, SQ = s(TOKENS), s(TOKENS), s(TOKENS)
    ms, rms = s(TILES), s(TILES)
    n = "l1_attn"
    qk_ready, dot_psum, lam_ready, scanned, squared = (c.sem(n + x) for x in ("_qk", "_dot_psum", "_decay", "_scanned", "_squared"))
    ms_psum, ms_ready, rms_ready, wo_ready, out_psum = (c.sem(n + x) for x in ("_ms_psum", "_ms", "_rms", "_wo", "_out_psum"))

    def tensor(pe, own):
        pe.wait_ge(qk_ready, 1)
        pe.wait_ge(c.loaded[n], 16)
        nc.tensor.matmul(PS[:, 2, 0:1], W["headsum"], qk, start=True, stop=True).then_inc(dot_psum, 1)
        pe.wait_ge(wo_ready, 1)
        for t in range(TILES):
            if t % 2 == 0:
                pe.wait_ge(scanned, t // 2 + 1)
            last = nc.tensor.matmul(PS[:, 6 + t // 4, (t % 4) * 128:(t % 4 + 1) * 128], O[:, 128 * t:128 * t + 128], WO, start=True, stop=True)
            if t % 4 == 3:
                last.then_inc(out_psum, 1)
        for t in range(TILES):
            if t % 4 == 0:
                pe.wait_ge(squared, t // 4 + 1)
            last = nc.tensor.matmul(PS[:, 3, t:t + 1], SQ[:, 128 * t:128 * t + 128], c.ones_row[:, 0:1], start=True, stop=True)
        last.then_inc(ms_psum, 1)

    def scalar(act, own):
        act.wait_ge(c.loaded[n], 16)
        act.wait_ge(c.sem("xt_ready"), 2 * k + 1)
        nc.scalar.activation(lam, W["log_decay"], ACT.Sigmoid).then_inc(lam_ready, 1)

    def vector(dve, own):
        dve.wait_ge(c.loaded[n], 16)
        nc.vector.tensor_tensor(qk, W["q"], W["k"], ALU.mult).then_inc(qk_ready, 1)
        nc.vector.tensor_scalar(WO, W["wo"], W["norm"], None, ALU.mult).then_inc(wo_ready, 1)
        dve.wait_ge(dot_psum, 1)
        own(nc.vector.tensor_copy(qks, PS[:, 2, 0:1]))
        own.settle()
        dve.wait_ge(lam_ready, 1)
        for b in range(B):
            sl = slice(256 * b, 256 * b + 256)
            dve.wait_ge(c.sem("xt_ready"), 2 * k + 1 + b // 2)
            own(nc.vector.tensor_scalar(V[:, sl], c.XT[:, sl], qks, None, ALU.mult))
            own.settle()
            nc.vector.tensor_tensor_scan(O[:, sl], lam.broadcast_to([128, 256]), V[:, sl], 0.0, ALU.mult, ALU.add).then_inc(scanned, 1)
        dve.wait_ge(ms_psum, 1)
        nc.vector.tensor_scalar(ms, PS[:, 3, 0:TILES], 1.0 / D, 1e-6, ALU.mult, ALU.add).then_inc(ms_ready, 1)
        dve.wait_ge(rms_ready, 1)
        dve.wait_ge(out_psum, 2)
        for t in range(TILES):
            own(nc.vector.scalar_tensor_tensor(c.X[:, t, :], PS[:, 6 + t // 4, (t % 4) * 128:(t % 4 + 1) * 128], rms[:, t:t + 1],
                                               c.X[:, t, :], ALU.mult, ALU.add))

    def gpsimd(pool, own):
        for half in range(HALVES):
            pool.wait_ge(scanned, 2 * half + 2)
            o = O[:, 512 * half:512 * half + 512]
            nc.gpsimd.tensor_tensor(SQ[:, 512 * half:512 * half + 512], o, o, ALU.mult).then_inc(squared, 1)
        pool.wait_ge(ms_ready, 1)
        nc.gpsimd.tensor_tensor(rms, ms, c.neghalf[:, 0:TILES], ALU.pow).then_inc(rms_ready, 1)

    return dict(tensor=tensor, scalar=scalar, vector=vector, gpsimd=gpsimd)


def l1_ffn(c, k):
    nc, W, PS, s = c.nc, c.W["l1_ffn"], c.PS, c.space
    N = 256
    n = "l1_ffn"
    idx = s(4, I32).rearrange("p (t j) -> p t j", t=2)
    idf = s(4).rearrange("p (t j) -> p t j", t=2)
    hit = s(32).rearrange("p (t j e) -> p t j e", t=2, j=2)
    C = s(16).rearrange("p (t e) -> p t e", t=2)
    parts = s(2 * 96, BF16).rearrange("p (t m) -> p t m", t=2)
    RT = s(N, BF16)[0:96, :]
    CT = s(N)[0:8, :]
    GA, UA, SG, H1, H2 = (s(2 * N).rearrange("p (r t) -> p r t", r=2) for _ in range(5))
    idx_loaded, parts_zero, parts_ready, rt_psum, rt_ready = (c.sem(n + x) for x in ("_idx", "_parts_zero", "_parts_ready", "_rt_psum", "_rt_ready"))
    gu_psum, gate_ready, sig_done, glu_done, hidden, down_done, out_psum = (c.sem(n + x) for x in (
        "_gate_up_psum", "_gate", "_sigmoid", "_glu", "_hidden", "_down", "_out_psum"))
    E = 8

    def sync(sp, own):
        sp.wait_ge(c.sem("xt_ready"), 2 * k + 1)
        sp.dma_start(idx.rearrange("p t j -> p (t j)"), c.ins["route"]).then_inc(idx_loaded, 16)

    def tensor(pe, own):
        pe.wait_ge(c.loaded[n], 16)
        pe.wait_ge(c.sem("xt_ready"), 2 * k + 2)

        def gate_up(e):
            if e >= 2:
                pe.wait_ge(hidden, e - 1)
            x = c.XT[:, 0:N]
            bank = PS[:, 2 + e % 2, :]
            nc.tensor.matmul(bank[:, 0:N], W["gate"][:, 128 * e:128 * e + 128], x, start=True, stop=True)
            nc.tensor.matmul(bank[:, N:2 * N], W["up"][:, 128 * e:128 * e + 128], x, start=True, stop=True)
            if e == 0:
                pe.wait_ge(parts_ready, 1)
                for t in range(2):
                    nc.tensor.transpose(PS[0:96, 0, 64 * t:64 * t + 64].bitcast(BF16), parts[:, t, :], c.identb).then_inc(rt_psum, 1)
                for t in range(2):
                    nc.tensor.transpose(PS[0:8, 1, 128 * t:128 * t + 128], C[:, t, :], c.ident).then_inc(rt_psum, 1)
                pe.wait_ge(rt_ready, 2)
            nc.tensor.matmul(PS[:, 4 + e % 2, 0:N], c.sel[0:96, e, :], RT, start=True, stop=True).then_inc(gu_psum, 1)

        def down(e):
            pe.wait_ge(hidden, e + 1)
            for t in range(2):
                nc.tensor.matmul(PS[:, 6, 128 * t:128 * t + 128], H2[:, e % 2, 128 * t:128 * t + 128], W["down"][:, 128 * e:128 * e + 128],
                                 start=e == 0 and t == 0, stop=False, skip_group_check=True).then_inc(down_done, 1)

        for e in range(E):
            gate_up(e)
            if e >= 1:
                down(e - 1)
        down(E - 1)
        for t in range(2):
            last = nc.tensor.matmul(PS[:, 6, 128 * t:128 * t + 128], CT[:, 128 * t:128 * t + 128], W["down_b"],
                                    start=False, stop=True, skip_group_check=True)
        last.then_inc(out_psum, 1)

    def scalar(act, own):
        act.wait_ge(rt_psum, 4)
        nc.scalar.copy(RT, PS[0:96, 0, 0:128].bitcast(BF16)).then_inc(rt_ready, 1)
        nc.scalar.copy(CT, PS[0:8, 1, 0:N]).then_inc(rt_ready, 1)
        for e in range(E):
            act.wait_ge(gate_ready, e + 1)
            if e >= 2:
                act.wait_ge(glu_done, e - 1)
            nc.scalar.activation(SG[:, e % 2, :], GA[:, e % 2, :], ACT.Sigmoid, scale=1.702).then_inc(sig_done, 1)

    def vector(dve, own):
        dve.wait_ge(idx_loaded, 16)
        dve.wait_ge(c.loaded[n], 16)
        dve.wait_ge(parts_zero, 1)
        own(nc.vector.tensor_copy(idf, idx))
        own.settle()
        own(nc.vector.tensor_scalar(idf, idf, -1.0, 8.0, ALU.mult, ALU.add))
        own.settle()
        for t in range(2):
            for j in range(2):
                own(nc.vector.tensor_scalar(hit[:, t, j, :], c.const["iota8"], idf[:, t, j:j + 1], None, ALU.is_equal))
        own.settle()
        own(nc.vector.tensor_tensor(C, hit[:, :, 0, :], hit[:, :, 1, :], ALU.add))
        own.settle()
        own(nc.vector.tensor_tensor(C, C, W["route_w"].rearrange("p (t e) -> p t e", t=2), ALU.mult))
        own.settle()
        route_parts(c, E, nc.vector, own, C, parts).then_inc(parts_ready, 1)

        def gate(e):
            dve.wait_ge(gu_psum, e + 1)
            if e >= 2:
                dve.wait_ge(glu_done, e - 1)
            nc.vector.tensor_scalar(GA[:, e % 2, :], PS[:, 2 + e % 2, 0:N], W["gate_b"][:, e:e + 1], 7.0, ALU.add, ALU.min).then_inc(gate_ready, 1)
            own(nc.vector.tensor_scalar(UA[:, e % 2, :], PS[:, 2 + e % 2, N:2 * N], W["up_b"][:, e:e + 1], 7.0, ALU.add, ALU.min))
            own.settle()
            own(nc.vector.tensor_scalar(UA[:, e % 2, :], UA[:, e % 2, :], -7.0, 1.0, ALU.max, ALU.add))
            own.settle()

        def glu(e):
            dve.wait_ge(glu_done, e + 1)
            own(nc.vector.tensor_tensor(H1[:, e % 2, :], H1[:, e % 2, :], UA[:, e % 2, :], ALU.mult))
            own.settle()
            if e >= 2:
                dve.wait_ge(down_done, 2 * (e - 1))
            nc.vector.tensor_tensor(H2[:, e % 2, :], PS[:, 4 + e % 2, 0:N], H1[:, e % 2, :], ALU.mult).then_inc(hidden, 1)

        for e in range(E):
            gate(e)
            if e >= 1:
                glu(e - 1)
        glu(E - 1)
        dve.wait_ge(out_psum, 1)
        own(nc.vector.tensor_tensor(c.X[:, 0:2, :], PS[:, 6, 0:256].rearrange("p (t d) -> p t d", d=D), c.X[:, 0:2, :], ALU.add))

    def gpsimd(pool, own):
        pool.wait_ge(c.sem("ln_var_ready"), TILES * (k + 1))
        nc.gpsimd.memset(parts, 0.0).then_inc(parts_zero, 1)
        for e in range(E):
            pool.wait_ge(sig_done, e + 1)
            if e >= 2:
                pool.wait_ge(hidden, e - 1)
            nc.gpsimd.tensor_tensor(H1[:, e % 2, :], GA[:, e % 2, :], SG[:, e % 2, :], ALU.mult).then_inc(glu_done, 1)

    return dict(sync=sync, tensor=tensor, scalar=scalar, vector=vector, gpsimd=gpsimd)


MAGIC = 12582912.0


def l2_ffn(c, k):
    nc, W, PS, s = c.nc, c.W["l2_ffn"], c.PS, c.space
    n = "l2_ffn"
    F = 512
    H = s(TILES * F).rearrange("p (t f) -> p t f", t=TILES)
    Hn = H[:, :, 0:D]
    T = s(TILES * F).rearrange("p (t f) -> p t f", t=TILES)
    Q = s(TILES * F, BF16).rearrange("p (t f) -> p t f", t=TILES)
    QT = s(TILES * F, BF16).rearrange("p (t f) -> p t f", t=TILES)
    WQ = s(2 * F, BF16).rearrange("p (i f) -> p i f", i=2)
    WT = s(2 * F).rearrange("p (i f) -> p i f", i=2)
    wsum, wmean, wscale = s(2), s(2), s(2)
    hi, lo, inv, step, lim = (s(TILES) for _ in range(5))
    stats, moments = s(TILES * 6).rearrange("p (t i) -> p t i", t=TILES), s(TILES * 2).rearrange("p (t i) -> p t i", t=TILES)
    var_ready, rstd_ready = c.sem(n + "_var"), c.sem(n + "_rstd")
    wsum_ready, wmean_psum, weights_ready = c.sem(n + "_wsum"), c.sem(n + "_wmean_psum"), c.sem(n + "_weights")
    q_ready, qt_psum, qt_ready, h_psum, h_ready, gelu_done, out_psum = (c.sem(n + x) for x in (
        "_q", "_qt_psum", "_qt", "_h_psum", "_h", "_gelu", "_out_psum"))
    scaled, rounded = c.sem(n + "_scaled"), c.sem(n + "_rounded")

    def tensor(pe, own):
        pe.wait_ge(wsum_ready, 2)
        nc.tensor.matmul(PS[:, 5, 0:2], c.ones_row, wsum, start=True, stop=True).then_inc(wmean_psum, 1)
        for t in range(TILES):
            pe.wait_ge(q_ready, 1)
            last = nc.tensor.transpose(PS[:, 4, 64 * t:64 * t + 64].bitcast(BF16), Q[:, t, 0:D], c.identb)
        last.then_inc(qt_psum, 1)
        pe.wait_ge(weights_ready, 2)
        pe.wait_ge(qt_ready, 1)
        for t in range(TILES):
            if t >= 4:
                pe.wait_ge(h_ready, t - 3)
            nc.tensor.matmul(PS[:, t % 4, :], QT[:, 0, 128 * t:128 * t + 128] if t < 4 else QT[:, 1, 128 * t - 512:128 * t - 384],
                             WQ[:, 0, :], start=True, stop=True).then_inc(h_psum, 1)
        for t in range(TILES):
            pe.wait_ge(q_ready, 2 + t // 4)
            pe.wait_ge(h_ready, TILES)
            if t >= 2:
                pe.wait_ge(qt_ready, t)
            for j in range(4):
                last = nc.tensor.transpose(PS[:, 4 + t % 2, 64 * j:64 * j + 64].bitcast(BF16), Q[:, t, 128 * j:128 * j + 128], c.identb)
            last.then_inc(qt_psum, 1)
            if t >= 1:
                second(pe, t - 1)
        second(pe, TILES - 1)

    def second(pe, t):
        pe.wait_ge(qt_ready, t + 2)
        for j in range(4):
            last = nc.tensor.matmul(PS[:, 6 + t // 4, (t % 4) * 128:(t % 4 + 1) * 128], QT[:, t, 128 * j:128 * j + 128],
                                    WQ[:, 1, 128 * j:128 * j + 128], start=j == 0, stop=j == 3)
        if t % 4 == 3:
            last.then_inc(out_psum, 1)

    def scalar(act, own):
        act.wait_ge(c.loaded[n], 16)
        act.wait_ge(c.sem("xt_ready"), 2 * k + 1)
        for i, w in enumerate(("w1", "w2")):
            nc.scalar.activation(WT[:, i, :], W[w], ACT.Abs, accum_out=wsum[:, i:i + 1]).then_inc(wsum_ready, 1)
        act.wait_ge(qt_psum, 1)
        nc.scalar.copy(QT[:, 0:2, :], PS[:, 4, :].bitcast(BF16).rearrange("p (i f) -> p i f", i=2)).then_inc(qt_ready, 1)
        for t in range(TILES):
            act.wait_ge(h_ready, t + 1)
            nc.scalar.activation(H[:, t, :], H[:, t, :], ACT.Gelu).then_inc(gelu_done, 1)
        for t in range(TILES):
            act.wait_ge(qt_psum, t + 2)
            nc.scalar.copy(QT[:, t, :], PS[:, 4 + t % 2, 0:256].bitcast(BF16)).then_inc(qt_ready, 1)

    def vector(dve, own):
        def norm(round_, src, dst, tiles):
            for t in tiles:
                own(nc.vector.bn_stats(stats[:, t, :], src[:, t, :]))
            own.settle()
            for t in tiles:
                nc.vector.bn_aggr(moments[:, t, :], stats[:, t, :]).then_inc(var_ready, 1)
            dve.wait_ge(rstd_ready, round_)
            for t in tiles:
                own(nc.vector.tensor_scalar(dst[:, t, :], src[:, t, :], moments[:, t, 0:1], c.rstd[:, t:t + 1], ALU.subtract, ALU.mult))
            own.settle()

        def quantise(h, tmp, q, t0, t1, weight):
            a, b = hi[:, t0:t1], lo[:, t0:t1]
            own(nc.vector.tensor_reduce(a, h, AX_X, ALU.max))
            own(nc.vector.tensor_reduce(b, h, AX_X, ALU.min))
            own.settle()
            own(nc.vector.scalar_tensor_tensor(lim[:, t0:t1], b, -1.0, a, ALU.mult, ALU.max))
            own.settle()
            own(nc.vector.tensor_scalar(lim[:, t0:t1], lim[:, t0:t1], 1e-5, None, ALU.max))
            own.settle()
            own(nc.vector.reciprocal(step[:, t0:t1], lim[:, t0:t1]))
            own(nc.vector.tensor_scalar(inv[:, t0:t1], lim[:, t0:t1], 1.0 / 127, wmean[:, weight:weight + 1], ALU.mult, ALU.mult))
            own.settle()
            own(nc.vector.tensor_scalar(step[:, t0:t1], step[:, t0:t1], 127.0, None, ALU.mult))
            own.settle()
            for t in range(t0, t1):
                own(nc.vector.tensor_scalar(tmp[:, t - t0, :], h[:, t - t0, :], step[:, t:t + 1], 127.0, ALU.mult, ALU.min))
            own.settle()
            own(nc.vector.tensor_scalar(tmp, tmp, -128.0, MAGIC, ALU.max, ALU.add))
            own.settle()
            return nc.vector.tensor_scalar(q, tmp, MAGIC, None, ALU.subtract)

        dve.wait_ge(c.loaded[n], 16)
        dve.wait_ge(c.sem("xn_ready"), TILES * (k + 1))
        norm(1, c.XN, Hn, range(TILES))
        dve.wait_ge(wmean_psum, 1)
        own(nc.vector.tensor_scalar(wmean, PS[:, 5, 0:2], 1.0 / (D * F), 1e-5, ALU.mult, ALU.max))
        own(nc.vector.tensor_tensor(Hn, Hn, bcast(W["ln1w"], 1, TILES), ALU.mult))
        own.settle()
        own(nc.vector.reciprocal(wscale, wmean))
        own(nc.vector.tensor_tensor(Hn, Hn, bcast(W["ln1b"], 1, TILES), ALU.add))
        own.settle()
        quantise(Hn, T[:, :, 0:D], Q[:, :, 0:D], 0, TILES, 0).then_inc(q_ready, 1)
        for i, w in enumerate(("w1", "w2")):
            own(nc.vector.tensor_scalar(WT[:, i, :], W[w], wscale[:, i:i + 1], 1.0, ALU.mult, ALU.min))
        own.settle()
        own(nc.vector.tensor_scalar(WT, WT, -1.0, MAGIC, ALU.max, ALU.add))
        own.settle()
        for i in range(2):
            nc.vector.tensor_scalar(WQ[:, i, :], WT[:, i, :], MAGIC, None, ALU.subtract).then_inc(weights_ready, 1)
        for t in range(TILES):
            dve.wait_ge(h_psum, t + 1)
            nc.vector.scalar_tensor_tensor(H[:, t, :], PS[:, t % 4, :], inv[:, t:t + 1], W["b1"], ALU.mult, ALU.add).then_inc(h_ready, 1)
        for half in range(HALVES):
            t0, t1 = 4 * half, 4 * half + 4
            h, tmp = H[:, t0:t1, :], T[:, t0:t1, :]
            dve.wait_ge(gelu_done, t1)
            norm(2 + half, H, H, range(t0, t1))
            own(nc.vector.tensor_tensor(h, h, bcast(W["ln2w"], 1, 4), ALU.mult))
            own.settle()
            own(nc.vector.tensor_tensor(h, h, bcast(W["ln2b"], 1, 4), ALU.add))
            own.settle()
            if half == 0:
                dve.wait_ge(qt_psum, 1)
            quantise(h, tmp, Q[:, t0:t1, :], t0, t1, 1).then_inc(q_ready, 1)
        own(nc.vector.tensor_tensor(c.X, c.X, bcast(W["b2"], 1, TILES), ALU.add))
        own.settle()
        for t in range(TILES):
            if t % 4 == 0:
                dve.wait_ge(out_psum, t // 4 + 1)
            own(nc.vector.scalar_tensor_tensor(c.X[:, t, :], PS[:, 6 + t // 4, (t % 4) * 128:(t % 4 + 1) * 128], inv[:, t:t + 1],
                                               c.X[:, t, :], ALU.mult, ALU.add))

    def gpsimd(pool, own):
        for r, (t0, t1) in enumerate(((0, TILES), (0, 4), (4, TILES))):
            pool.wait_ge(var_ready, (8, 12, 16)[r])
            own(nc.gpsimd.tensor_scalar(c.var_eps[:, t0:t1], moments[:, t0:t1, 1], 1e-5, None, ALU.add))
            own.settle()
            nc.gpsimd.tensor_tensor(c.rstd[:, t0:t1], c.var_eps[:, t0:t1], c.neghalf[:, t0:t1], ALU.pow).then_inc(rstd_ready, 1)

    return dict(tensor=tensor, scalar=scalar, vector=vector, gpsimd=gpsimd)


def l3_xattn(c, k):
    nc, W, PS, s = c.nc, c.W["l3_xattn"], c.PS, c.space
    n = "l3_xattn"
    ON_POOL = (1, 3, 4, 6, 7)
    NP = len(ON_POOL)
    QX, KX, VX, O, OT = (s(TOKENS) for _ in range(5))
    PR = s(4 * 2048).rearrange("p (r m) -> p r m", r=4)
    E = s(TILES * 256).rearrange("p (t m) -> p t m", t=TILES)
    mx, den = s(128), s(128)
    k_psum, v_psum, q_psum, copied = (c.sem(n + x) for x in ("_k_psum", "_v_psum", "_q_psum", "_copied"))
    multiplied, summed, shifted, exp_done, weights_ready = (c.sem(n + x) for x in ("_multiplied", "_summed", "_shifted", "_exp", "_probs"))
    var_ready, rstd_ready, on_ready, ot_psum, ot_ready, out_psum = (c.sem(n + x) for x in (
        "_var", "_rstd", "_on", "_ot_psum", "_ot", "_out_psum"))
    heads = lambda a, t: a[:, 128 * t:128 * t + 128].rearrange("p (h d) -> p h d", d=8)

    def tensor(pe, own):
        pe.wait_ge(c.loaded[n], 16)
        pe.wait_ge(c.sem("xt_ready"), 2 * k + 2)
        wq, wk, wv = (2, c.XT, "wq", "bq", q_psum), (4, c.CTXT, "wk", "bk", k_psum), (6, c.CTXT, "wv", "bv", v_psum)
        for (bank, src, w, b, done), half in ((wq, 0), (wk, 0), (wq, 1), (wk, 1), (wv, 0), (wv, 1)):
            for t in range(4 * half, 4 * half + 4):
                out = PS[:, bank + t // 4, (t % 4) * 128:(t % 4 + 1) * 128]
                nc.tensor.matmul(out, src[:, 128 * t:128 * t + 128], W[w], start=True, stop=False)
                last = nc.tensor.matmul(out, c.ones_row[0:1, :], W[b], start=False, stop=True)
                if t % 4 == 3:
                    last.then_inc(done, 1)
        for t in range(TILES):
            pe.wait_ge(on_ready, t + 1)
            nc.tensor.transpose(PS[:, t // 4, (t % 4) * 128:(t % 4 + 1) * 128], O[:, 128 * t:128 * t + 128], c.ident).then_inc(ot_psum, 1)
        for t in range(TILES):
            pe.wait_ge(ot_ready, t // 4 + 1)
            out = PS[:, 6 + t // 4, (t % 4) * 128:(t % 4 + 1) * 128]
            nc.tensor.matmul(out, OT[:, 128 * t:128 * t + 128], W["wo"], start=True, stop=False)
            last = nc.tensor.matmul(out, c.ones_row[0:1, :], W["bo"], start=False, stop=True)
            if t % 4 == 3:
                last.then_inc(out_psum, 1)

    def scalar(act, own):
        q, kk, v = (2, QX, q_psum), (4, KX, k_psum), (6, VX, v_psum)
        for (bank, dst, ready), half in ((q, 0), (kk, 0), (q, 1), (kk, 1), (v, 0), (v, 1)):
            act.wait_ge(ready, half + 1)
            nc.scalar.copy(dst[:, 512 * half:512 * half + 512], PS[:, bank + half, :]).then_inc(copied, 1)
        for half in range(HALVES):
            act.wait_ge(shifted, half + 1)
            e = E[:, 4 * half:4 * half + 4, :]
            nc.scalar.activation(e, e, ACT.Exp, scale=1.0 / math.sqrt(128.0)).then_inc(exp_done, 1)
        for half in range(HALVES):
            act.wait_ge(ot_psum, 4 * half + 4)
            nc.scalar.activation(OT[:, 512 * half:512 * half + 512], PS[:, half, :], ACT.Identity,
                                 bias=W["ln_b"], scale=W["ln_g"]).then_inc(ot_ready, 1)

    def score_products(engine, t):
        return engine.tensor_tensor(PR[:, t % 4, :].rearrange("p (h g d) -> p h g d", h=16, g=16), bcast(heads(QX, t), 2, 16),
                                    bcast(heads(KX, t), 1, 16), ALU.mult)

    def value_products(engine, t):
        return engine.tensor_tensor(PR[:, t % 4, :].rearrange("p (h d g) -> p h d g", h=16, d=8),
                                    bcast(E[:, t, :].rearrange("p (h g) -> p h g", h=16), 2, 8),
                                    bcast(heads(VX, t).rearrange("p g d -> p d g"), 1, 16), ALU.mult)

    def gpsimd(pool, own):
        for t in ON_POOL:
            pool.wait_ge(copied, 2 * (t // 4) + 2)
            if t >= 4:
                pool.wait_ge(summed, t - 3)
            score_products(nc.gpsimd, t).then_inc(multiplied, 1)
        for t in ON_POOL:
            pool.wait_ge(copied, 5 + t // 4)
            pool.wait_ge(exp_done, t // 4 + 1)
            pool.wait_ge(summed, TILES + t - 3)
            value_products(nc.gpsimd, t).then_inc(multiplied, 1)
        pool.wait_ge(var_ready, TILES)
        own(nc.gpsimd.tensor_scalar(c.var_eps[:, 0:TILES], c.moments[:, :, 1], 1e-5, None, ALU.add))
        own.settle()
        nc.gpsimd.tensor_tensor(c.rstd[:, 0:TILES], c.var_eps[:, 0:TILES], c.neghalf[:, 0:TILES], ALU.pow).then_inc(rstd_ready, 1)

    def vector(dve, own):
        def softmax(half):
            e = E[:, 4 * half:4 * half + 4, :].rearrange("p t (h g) -> p (t h) g", g=16)
            m = mx[:, 64 * half:64 * half + 64]
            dve.wait_ge(summed, 4 * half + 4)
            own(nc.vector.tensor_reduce(m, e, AX_X, ALU.max))
            own.settle()
            nc.vector.tensor_tensor(e, e, bcast(m, 2, 16), ALU.subtract).then_inc(shifted, 1)

        for t in range(TILES):
            if t in ON_POOL:
                dve.wait_ge(multiplied, ON_POOL.index(t) + 1)
            else:
                dve.wait_ge(copied, 2 * (t // 4) + 2)
                own(score_products(nc.vector, t))
                own.settle()
            nc.vector.tensor_reduce(E[:, t, :], PR[:, t % 4, :].rearrange("p (m d) -> p m d", d=8), AX_X, ALU.add).then_inc(summed, 1)
            if t % 4 == 3:
                softmax(t // 4)
        for half in range(HALVES):
            dve.wait_ge(exp_done, half + 1)
            d = den[:, 64 * half:64 * half + 64]
            own(nc.vector.tensor_reduce(d, E[:, 4 * half:4 * half + 4, :].rearrange("p t (h g) -> p (t h) g", g=16), AX_X, ALU.add))
        own.settle()
        own(nc.vector.reciprocal(den, den))
        own.settle()
        for t in range(TILES):
            if t in ON_POOL:
                dve.wait_ge(multiplied, NP + ON_POOL.index(t) + 1)
            else:
                dve.wait_ge(copied, 5 + t // 4)
                own(value_products(nc.vector, t))
                own.settle()
            nc.vector.tensor_reduce(O[:, 128 * t:128 * t + 128], PR[:, t % 4, :].rearrange("p (m g) -> p m g", g=16), AX_X, ALU.add).then_inc(summed, 1)
        dve.wait_ge(summed, 2 * TILES)
        o = O.rearrange("p (m d) -> p m d", d=8)
        own(nc.vector.tensor_tensor(o, o, bcast(den, 2, 8), ALU.mult))
        own.settle()
        for t in range(TILES):
            own(nc.vector.bn_stats(c.stats[:, t, :], O[:, 128 * t:128 * t + 128]))
        own.settle()
        for t in range(TILES):
            nc.vector.bn_aggr(c.moments[:, t, :], c.stats[:, t, :]).then_inc(var_ready, 1)
        dve.wait_ge(rstd_ready, 1)
        for t in range(TILES):
            nc.vector.tensor_scalar(O[:, 128 * t:128 * t + 128], O[:, 128 * t:128 * t + 128], c.moments[:, t, 0:1], c.rstd[:, t:t + 1],
                                    ALU.subtract, ALU.mult).then_inc(on_ready, 1)
        c.add(n)(dve, own)

    return dict(tensor=tensor, scalar=scalar, vector=vector, gpsimd=gpsimd)


def l1_xattn(c, k):
    nc, W, PS, s = c.nc, c.W["l1_xattn"], c.PS, c.space
    n = "l1_xattn"
    WINDOW, KD, R, HR = 3, 32, 64, 32
    SCALE = 1.0 / math.sqrt(128.0)
    KVT = s(TOKENS)[0:KD, :]
    KTAB = s(TILES * 96).rearrange("p (t e) -> p t e", t=TILES)
    KM = s(2 * TILES * 64).rearrange("p (i t e) -> p i t e", i=2, t=TILES)
    A = s(16 * KD)[0:48, :]
    W2 = s(4 * 128).rearrange("p (i d) -> p i d", i=4)
    QC = s(TOKENS)[0:48, :]
    OV = c.annex(TILES * 512).rearrange("p (t m) -> p t m", t=TILES)
    segs = OV.rearrange("p t m -> p (t m)")
    SEGI, SEG, BAD, BAD2 = segs[:, 0:1024].bitcast(I32), segs[:, 1024:2048], segs[:, 2048:3072], segs[:, 3072:4096]
    OH = s(2 * 2 * WINDOW * 256).rearrange("p (r c j t) -> p r c j t", r=2, c=2, j=WINDOW)
    KG = s(TILES * WINDOW * 96).rearrange("p (t j e) -> p t j e", t=TILES, j=WINDOW)
    KC, KSN = (s(WINDOW * 64).rearrange("p (j e) -> p j e", j=WINDOW) for _ in range(2))
    QPR = s(4 * 16 * 96)
    Q, PR = (QPR[:, 3072 * i:3072 * i + 3072].rearrange("p (r h e) -> p r h e", r=2, h=16) for i in range(2))
    VP = QPR[:, 0:TILES * 512].rearrange("p (t m) -> p t m", t=TILES)
    T1 = QPR[:, TILES * 512:TILES * 512 + 1024].rearrange("p (r m) -> p r m", r=2)
    PR0 = s(16 * 96).rearrange("p (h e) -> p h e", h=16)
    SC = s(TILES * WINDOW * 16).rearrange("p (t j h) -> p t j h", t=TILES, j=WINDOW)
    segt_i, segt = s(TILES, I32), s(TILES)
    VM, VT = (s(TILES * WINDOW).rearrange("p (t j) -> p t j", t=TILES) for _ in range(2))
    mx, den = (s(TILES * 16).rearrange("p (t h) -> p t h", t=TILES) for _ in range(2))
    OTc = s(2048).rearrange("p (i t) -> p i t", i=4)
    sem = lambda x: c.sem(n + x)
    seg_loaded, kv_psum, kv_ready, absorb_psum, absorb_ready, qc_psum, qc_ready = (sem(x) for x in (
        "_seg", "_kv_psum", "_kv", "_absorb_psum", "_absorb", "_qc_psum", "_qc"))
    ktab_psum, ktab_ready, onehot, kg_psum, kg_ready, oh_used = (sem(x) for x in ("_ktab_psum", "_ktab", "_onehot", "_kg_psum", "_kg", "_oh_used"))
    q_psum, q_ready, kg_rotated, prod, summed = (sem(x) for x in ("_q_psum", "_q", "_kg_rotated", "_prod", "_sum"))
    exp_ready, exp_done, ov_ready, ot_psum, ot_ready, out_psum = (sem(x) for x in ("_shifted", "_exp", "_ov", "_ot_psum", "_ot", "_out_psum"))
    probs_ready, part_ready = sem("_probs"), sem("_part")

    def sync(sp, own):
        sp.wait_ge(c.sem("xt_ready"), 2 * k + 1)
        sp.dma_start(SEGI, c.ins["seg"].broadcast_to([128, TOKENS])).then_inc(seg_loaded, 16)
        sp.dma_start(segt_i, c.ins["seg_rows"]).then_inc(seg_loaded, 16)

    def tensor(pe, own):
        pe.wait_ge(c.loaded[n], 16)
        pe.wait_ge(c.sem("xt_ready"), 2 * k + 2)
        for half in range(HALVES):
            sl = slice(512 * half, 512 * half + 512)
            nc.tensor.matmul(PS[0:KD, 2 + half, :], W["kv_comp"], c.CTXT[:, sl], start=True, stop=True).then_inc(kv_psum, 1)
        for half in range(HALVES):
            sl = slice(512 * half, 512 * half + 512)
            nc.tensor.matmul(PS[0:48, 4 + half, :], W["q_down"], c.XT[:, sl], start=True, stop=True).then_inc(qc_psum, 1)
        for h in range(16):
            last = nc.tensor.matmul(PS[0:48, 6, KD * h:KD * h + KD], W["q_upT"][:, 48 * h:48 * h + 48], W["k_upT"][:, KD * h:KD * h + KD],
                                    start=True, stop=True)
        last.then_inc(absorb_psum, 1)
        for h in range(16):
            last = nc.tensor.matmul(PS[32 * (h % 4):32 * (h % 4) + 32, 7, 128 * (h // 4):128 * (h // 4) + 128],
                                    W["v_upT"][:, KD * h:KD * h + KD], W["out"][:, 128 * h:128 * h + 128], start=True, stop=True)
        last.then_inc(absorb_psum, 1)
        pe.wait_ge(kv_ready, 2)
        for t in range(TILES):
            nc.tensor.matmul(PS[:, 0, 64 * t:64 * t + 64], KVT[:, 128 * t:128 * t + 128], W["k_rope"], start=True, stop=True)
        for t in range(TILES):
            last = nc.tensor.matmul(PS[:, 1, KD * t:KD * t + KD], c.CTXT[:, 128 * t:128 * t + 128], W["kv_comp"], start=True, stop=True)
        last.then_inc(ktab_psum, 1)

        def gather(t):
            b = t // 2
            if t % 2 == 0:
                pe.wait_ge(onehot, b + 1)
            if t == 0:
                pe.wait_ge(ktab_ready, 2)
            pe.wait_ge(qc_ready, 2)
            pe.wait_ge(absorb_ready, 2)
            if t >= 2:
                pe.wait_ge(kg_ready, t - 1)
            for j in range(WINDOW):
                for kc in range(2):
                    last = nc.tensor.matmul(PS[:, 6 + t % 2, 96 * j:96 * j + 96], OH[:, b % 2, kc, j, 128 * (t % 2):128 * (t % 2) + 128],
                                            KTAB[:, 2 * b + kc, :], start=kc == 0, stop=kc == 1)
            last.then_inc(kg_psum, 1)

        def queries(t):
            r = 3 * (t % 2)
            if t == 0:
                pe.wait_ge(ktab_ready, 2)
            if t >= 2:
                pe.wait_ge(q_ready, 2 * (t - 1))
            x = QC[:, 128 * t:128 * t + 128]
            for half in range(2):
                nc.tensor.matmul(PS[:, r + half, :], x, W["q_rope"][:, 512 * half:512 * half + 512], start=True, stop=True)
            nc.tensor.matmul(PS[:, r + 2, :], x, A, start=True, stop=True).then_inc(q_psum, 1)

        for t in range(TILES):
            gather(t)
            queries(t)
        for half in range(HALVES):
            for i in range(4):
                b0 = i
                if half == 1:
                    pe.wait_ge(ot_ready, i + 1)
                for t in range(4 * half, 4 * half + 4):
                    if i == 0:
                        pe.wait_ge(ov_ready, t + 1)
                        pe.wait_ge(part_ready, t + 1)
                    out, chunk = PS[:, b0, (t % 4) * 128:(t % 4 + 1) * 128], slice(128 * i, 128 * i + 128)
                    nc.tensor.matmul(out, OV[:, t, chunk], c.ident, start=True, stop=False)
                    last = nc.tensor.matmul(out, VP[:, t, chunk], c.ident, start=False, stop=True)
                last.then_inc(ot_psum, 1)
            pe.wait_ge(ot_ready, 4 * half + 4)
            for t in range(4):
                for i in range(4):
                    last = nc.tensor.matmul(PS[:, 6 + half, 128 * t:128 * t + 128], OTc[:, i, 128 * t:128 * t + 128], W2[:, i, :],
                                            start=i == 0, stop=i == 3)
            last.then_inc(out_psum, 1)

    def scalar(act, own):
        for half in range(HALVES):
            act.wait_ge(kv_psum, half + 1)
            nc.scalar.copy(KVT[:, 512 * half:512 * half + 512], PS[0:KD, 2 + half, :]).then_inc(kv_ready, 1)
        for half in range(HALVES):
            act.wait_ge(qc_psum, half + 1)
            nc.scalar.copy(QC[:, 512 * half:512 * half + 512], PS[0:48, 4 + half, :]).then_inc(qc_ready, 1)
        act.wait_ge(absorb_psum, 2)
        nc.scalar.copy(A, PS[0:48, 6, :]).then_inc(absorb_ready, 1)
        nc.scalar.copy(W2, PS[:, 7, :].rearrange("p (i d) -> p i d", i=4)).then_inc(absorb_ready, 1)
        act.wait_ge(ktab_psum, 1)
        nc.scalar.copy(KTAB[:, :, 64:96], PS[:, 1, 0:256].rearrange("p (t e) -> p t e", t=TILES)).then_inc(ktab_ready, 1)
        for t in range(TILES):
            act.wait_ge(kg_psum, t + 1)
            nc.scalar.copy(KG[:, t, :, :], PS[:, 6 + t % 2, 0:288].rearrange("p (j e) -> p j e", j=WINDOW)).then_inc(kg_ready, 1)
            act.wait_ge(q_psum, t + 1)
            if t >= 2:
                act.wait_ge(prod, 2 * (t - 1))
                act.wait_ge(summed, WINDOW * (t - 2) + 1)
            nc.scalar.copy(Q[:, t % 2, :, 0:64],
                           PS[:, 3 * (t % 2):3 * (t % 2) + 2, :].rearrange("p b (h e) -> p (b h) e", e=64)).then_inc(q_ready, 1)
            nc.scalar.copy(Q[:, t % 2, :, 64:96], PS[:, 3 * (t % 2) + 2, :].rearrange("p (h e) -> p h e", h=16)).then_inc(q_ready, 1)
        act.wait_ge(exp_ready, 1)
        nc.scalar.activation(SC, SC, ACT.Exp, scale=SCALE).then_inc(exp_done, 1)
        for half in range(HALVES):
            for i in range(4):
                act.wait_ge(ot_psum, 4 * half + i + 1)
                if half == 1 and i == 0:
                    act.wait_ge(out_psum, 1)
                nc.scalar.copy(OTc[:, i, :], PS[:, i, :]).then_inc(ot_ready, 1)

    def vector(dve, own):
        dve.wait_ge(ktab_psum, 1)
        kr = PS[:, 0, :].rearrange("p (t i e) -> p t i e", t=TILES, i=2)
        cos, sin = (c.const[x].rearrange("p (t e) -> p t e", t=TILES) for x in ("rope_c", "rope_s"))
        own(nc.vector.tensor_tensor(KM[:, 0, :, :].rearrange("p t (i e) -> p t i e", i=2), kr, bcast(cos, 2, 2), ALU.mult))
        own(nc.vector.tensor_tensor(KM[:, 1, :, :].rearrange("p t (i e) -> p t i e", i=2), kr, bcast(sin, 2, 2), ALU.mult))
        own.settle()
        own(nc.vector.tensor_tensor(KTAB[:, :, 0:32], KM[:, 0, :, 0:32], KM[:, 1, :, 32:64], ALU.subtract))
        nc.vector.tensor_tensor(KTAB[:, :, 32:64], KM[:, 0, :, 32:64], KM[:, 1, :, 0:32], ALU.add).then_inc(ktab_ready, 1)
        own.settle()
        dve.wait_ge(seg_loaded, 32)
        own(nc.vector.tensor_copy(SEG, SEGI))
        own(nc.vector.tensor_copy(segt, segt_i))
        own.settle()
        own(nc.vector.tensor_scalar(BAD, SEG, 0.0, 1.0 / L, ALU.is_lt, ALU.mult))
        own(nc.vector.tensor_scalar(BAD2, SEG, L + WINDOW - 2 + 0.0, 1.0 / L, ALU.is_gt, ALU.mult))
        for j in range(WINDOW):
            own(nc.vector.tensor_scalar(VM[:, :, j], segt, float(j), None, ALU.is_ge))
            own(nc.vector.tensor_scalar(VT[:, :, j], segt, float(L - 1 + j), None, ALU.is_le))
        own.settle()
        own(nc.vector.tensor_tensor(BAD, BAD, BAD2, ALU.add))
        own(nc.vector.tensor_tensor(VM, VM, VT, ALU.mult))
        own.settle()
        own(nc.vector.tensor_scalar(VM, VM, 1.0, -MASKED, ALU.subtract, ALU.mult))

        def onehots(b):
            if b >= 2:
                dve.wait_ge(kg_psum, 2 * b - 2)
            for kc in range(2):
                for j in range(WINDOW):
                    sl = slice(256 * b, 256 * b + 256)
                    last = nc.vector.scalar_tensor_tensor(OH[:, b % 2, kc, j, :], SEG[:, sl], c.const["key_index"][:, 3 * kc + j:3 * kc + j + 1],
                                                          BAD[:, sl], ALU.is_equal, ALU.add)
                    if (kc, j) != (1, WINDOW - 1):
                        own(last)
            own.settle()
            last.then_inc(onehot, 1)

        def rotate(t):
            dve.wait_ge(kg_ready, t + 1)
            if t >= 1:
                dve.wait_ge(kg_rotated, t)
            kg = KG[:, t, :, 0:64].rearrange("p j (i e) -> p j i e", i=2)
            for dst, table in ((KC, "rope_c"), (KSN, "rope_s")):
                tb = bcast(bcast(c.const[table][:, 32 * t:32 * t + 32], 1, 2), 1, WINDOW)
                own(nc.vector.tensor_tensor(dst.rearrange("p j (i e) -> p j i e", i=2), kg, tb, ALU.mult))
            own.settle()
            own(nc.vector.tensor_tensor(KG[:, t, :, 0:32], KC[:, :, 0:32], KSN[:, :, 32:64], ALU.add))
            nc.vector.tensor_tensor(KG[:, t, :, 32:64], KC[:, :, 32:64], KSN[:, :, 0:32], ALU.subtract).then_inc(kg_rotated, 1)
            own.settle()

        def sums(t):
            dve.wait_ge(q_ready, 2 * t + 2)
            dve.wait_ge(kg_rotated, t + 1)
            if t >= 1:
                dve.wait_ge(summed, WINDOW * (t - 1) + 1)
            own(nc.vector.tensor_tensor(PR0, Q[:, t % 2, :, :], bcast(KG[:, t, 0, :], 1, 16), ALU.mult))
            own.settle()
            nc.vector.tensor_reduce(SC[:, t, 0, :], PR0, AX_X, ALU.add).then_inc(summed, 1)
            for j in range(1, WINDOW):
                dve.wait_ge(prod, 2 * t + j)
                nc.vector.tensor_reduce(SC[:, t, j, :], PR[:, j - 1, :, :], AX_X, ALU.add).then_inc(summed, 1)

        own.settle()
        onehots(0)
        onehots(1)
        rotate(0)
        for t in range(TILES):
            if t + 1 < TILES:
                rotate(t + 1)
            sums(t)
            if t in (1, 3):
                onehots(t // 2 + 2)
        dve.wait_ge(summed, WINDOW * TILES)
        own.settle()
        own(nc.vector.tensor_tensor(SC, SC, bcast(VM, 3, 16), ALU.add))
        own.settle()
        own(nc.vector.tensor_tensor(mx, SC[:, :, 0, :], SC[:, :, 1, :], ALU.max))
        own.settle()
        own(nc.vector.tensor_tensor(mx, mx, SC[:, :, 2, :], ALU.max))
        own.settle()
        nc.vector.tensor_tensor(SC, SC, bcast(mx, 2, WINDOW), ALU.subtract).then_inc(exp_ready, 1)
        dve.wait_ge(exp_done, 1)
        own(nc.vector.tensor_tensor(den, SC[:, :, 0, :], SC[:, :, 1, :], ALU.add))
        own.settle()
        own(nc.vector.tensor_tensor(den, den, SC[:, :, 2, :], ALU.add))
        own.settle()
        own(nc.vector.reciprocal(den, den))
        own.settle()
        nc.vector.tensor_tensor(SC, SC, bcast(den, 2, WINDOW), ALU.mult).then_inc(probs_ready, 1)
        dve.wait_ge(probs_ready, 1)
        for t in range(TILES):
            ov = OV[:, t, :].rearrange("p (h e) -> p h e", e=KD)
            t1 = T1[:, t % 2, :].rearrange("p (h e) -> p h e", e=KD)
            if t >= 2:
                dve.wait_ge(ov_ready, t - 1)
            own(nc.vector.tensor_tensor(ov, bcast(SC[:, t, 0, :], 2, KD), bcast(KG[:, t, 0, 64:96], 1, 16), ALU.mult))
            own(nc.vector.tensor_tensor(t1, bcast(SC[:, t, 1, :], 2, KD), bcast(KG[:, t, 1, 64:96], 1, 16), ALU.mult))
            own.settle()
            nc.vector.tensor_tensor(ov, ov, t1, ALU.add).then_inc(ov_ready, 1)
        c.add(n)(dve, own)

    def gpsimd(pool, own):
        for t in range(TILES):
            pool.wait_ge(q_ready, 2 * t + 2)
            pool.wait_ge(kg_rotated, t + 1)
            for j in range(1, WINDOW):
                if t >= 1:
                    pool.wait_ge(summed, WINDOW * (t - 1) + j + 1)
                nc.gpsimd.tensor_tensor(PR[:, j - 1, :, :], Q[:, t % 2, :, :], bcast(KG[:, t, j, :], 1, 16), ALU.mult).then_inc(prod, 1)
        pool.wait_ge(probs_ready, 1)
        for t in range(TILES):
            nc.gpsimd.tensor_tensor(VP[:, t, :].rearrange("p (h e) -> p h e", e=KD), bcast(SC[:, t, 2, :], 2, KD),
                                    bcast(KG[:, t, 2, 64:96], 1, 16), ALU.mult).then_inc(part_ready, 1)

    return dict(sync=sync, tensor=tensor, scalar=scalar, vector=vector, gpsimd=gpsimd)


def l3_attn(c, k):
    nc, W, PS, s = c.nc, c.W["l3_attn"], c.PS, c.space
    n = "l3_attn"
    HD, LAG3 = 64, 21
    QT, KT = (s(3 * 2048).rearrange("p (r g t) -> p r g t", r=3, g=8) for _ in range(2))
    VB = s(2 * 2 * 16 * 65).rearrange("p (r c h e) -> p r c h e", r=2, c=2, h=16)
    ON = c.annex(2 * 2 * 1024).rearrange("p (r t m) -> p r t m", r=2, t=2)
    OT = c.annex(1024).rearrange("p (i t) -> p i t", i=8)
    MTR = s(2 * 8 * 256, BF16).rearrange("p (r g t) -> p r g t", r=2, g=8)
    bqs = s(8)
    work, P = attention_work(c, 2, ring=3)
    filled, free = c.sem(n + "_bank7_filled"), c.sem(n + "_bank7_free")
    fills, bias_ready = c.sem(n + "_fills"), c.sem(n + "_bias")
    bout_psum, bout_ready, bout = c.sem(n + "_bout_psum"), c.sem(n + "_bout"), s(128)[0:1, :]

    jobs = []
    for b in range(B):
        for i in range(4):
            jobs.append((16 * (b - 1) + 5 + 2 * i if b else -1, "q", b, i))
            jobs.append((16 * (b - 1) + 6 + 2 * i if b else -1, "k", b, i))
        for i in range(4):
            jobs.append((16 * (b - 1) + 29 + i if b else -1, "v", b, i))
        for i in range(6):
            last = b == B - 1
            jobs.append((16 * b + (41 if last else 47) + i + (0 if last else i // 3), ("t", "t", "o")[i % 3], b, i))
    jobs.sort(key=lambda j: j[0])
    FIRST = sum(j[0] < 0 for j in jobs)
    STEPS = max(j[0] for j in jobs) + 1
    where = lambda j: PS[:, j % 8 if j < FIRST else 7, :]

    def run_job(pe, j):
        step, kind, b, i = jobs[j]
        bank = where(j)
        if j >= FIRST:
            pe.wait_ge(free, j)
            if step > 18:
                pe.wait_ge(c.sem(n + "_maxT_ready"), min(B, (step - 3) // 16))
        elif j >= 8:
            pe.wait_ge(free, j - 7)
        if kind in "qk":
            w = W["w" + kind]
            for g in (2 * i, 2 * i + 1):
                last = nc.tensor.matmul(bank[:, 256 * (g % 2):256 * (g % 2) + 256], w[:, 128 * g:128 * g + 128],
                                        c.XT[:, 256 * b:256 * b + 256], start=True, stop=True)
        elif kind == "v":
            kc, half = i // 2, i % 2
            last = nc.tensor.matmul(bank, c.XT[:, 256 * b + 128 * kc:256 * b + 128 * kc + 128], W["wv"][:, 512 * half:512 * half + 512],
                                    start=True, stop=True)
        elif kind == "t":
            if i % 3 == 0:
                pe.wait_ge(c.sem(n + "_norm_done"), 8 * (b + 1))
            for m in range(4):
                ch = 4 * (i % 3) + m
                last = nc.tensor.transpose(bank[:, 128 * m:128 * m + 128], ON[:, b % 2, i // 3, 128 * ch:128 * ch + 128], c.ident)
        else:
            for ch in range(8):
                nc.tensor.matmul(bank[:, 0:128], OT[:, ch, :], W["wo"][:, 128 * ch:128 * ch + 128], start=ch == 0, stop=False)
            last = nc.tensor.matmul(bank[:, 0:128], c.ones_row[0:1, :], bout, start=False, stop=True)
        last.then_inc(filled, 1)

    def leave(act, j):
        step, kind, b, i = jobs[j]
        if kind == "o":
            return
        bank = where(j)
        act.wait_ge(filled, j + 1)
        if kind in "qk":
            for g in (2 * i, 2 * i + 1):
                ps = bank[:, 256 * (g % 2):256 * (g % 2) + 256]
                if kind == "q":
                    ins = nc.scalar.activation(QT[:, b % 3, g, :], ps, ACT.Identity, bias=bqs[:, g:g + 1], scale=HD ** -0.5)
                else:
                    ins = nc.scalar.activation(KT[:, b % 3, g, :], ps, ACT.Identity, bias=W["bk"][:, g:g + 1])
        elif kind == "v":
            ins = nc.scalar.copy(VB[:, b % 2, i // 2, 8 * (i % 2):8 * (i % 2) + 8, 0:HD], bank.rearrange("p (h e) -> p h e", e=HD))
        else:
            ins = nc.scalar.copy(OT[:, 4 * (i % 3):4 * (i % 3) + 4, :], bank.rearrange("p (m t) -> p m t", m=4))
        ins.then_inc(free, 1)

    def at(step):
        return [j for j in range(len(jobs)) if jobs[j][0] == step]

    def max_scores(b, h, bank):
        r, g = 64 * (h % 2), h // 2
        q, kk = QT[r:r + 64, b % 3, g, :], KT[r:r + 64, b % 3, g, :]
        nc.tensor.matmul(bank[:, 0:256], q[:, 0:128], kk, start=True, stop=True)
        return nc.tensor.matmul(bank[:, 256:512], q[:, 128:256], kk, start=True, stop=True)

    def exp_scores(b, h, bank):
        r, g = 64 * (h % 2), h // 2
        q, kk = QT[r:r + 64, b % 3, g, :], KT[r:r + 64, b % 3, g, :]
        for kc in range(2):
            out = bank[:, 256 * kc:256 * kc + 256]
            nc.tensor.matmul(out, kk[:, 128 * kc:128 * kc + 128], q, start=True, stop=False)
            last = nc.tensor.matmul(out, c.ones3[r:r + 64, :], MTR[r:r + 64, b % 2, g, :], start=False, stop=True)
        return last

    def place_max(sp, b, placed):
        for part in range(3):
            for r in range(2):
                sp.dma_start(MTR[64 * r + part:64 * r + part + 1, b % 2, :, :], work[3][16 * part + 8 * r:16 * part + 8 * r + 8, :]).then_inc(placed, 16)
    place_max.dmas = 6

    def start_batch(pe, b):
        if b > 0:
            pe.wait_ge(free, 1 + max(j for j in range(len(jobs)) if jobs[j][1] in "qk" and jobs[j][2] == b))

    def extra_tensor(pe, step):
        for j in at(step):
            run_job(pe, j)

    def before_max(pe, step):
        done = [j for j in range(len(jobs)) if jobs[j][0] <= step]
        pe.wait_ge(free, len(done))

    def extra_scalar(act, step):
        for j in at(step):
            leave(act, j)

    def extra_vector(dve, own, step):
        for j in at(step):
            if jobs[j][1] == "o":
                _, _, b, i = jobs[j]
                t = 2 * b + i // 3
                dve.wait_ge(filled, j + 1)
                nc.vector.tensor_tensor(c.X[:, t, :], where(j)[:, 0:128], c.X[:, t, :], ALU.add).then_inc(free, 1)

    def values(b, kc, h):
        return VB[:, b % 2, kc, h, :]

    main, _ = attention(c, n, max_scores=max_scores, exp_scores=exp_scores, values=values, place_max=place_max, dv=HD,
                        heads_a_bank=2, P=P, work=work, start_batch=start_batch, head_order=lambda h: (h % 2) * 8 + h // 2,
                        extra=dict(tensor=extra_tensor, scalar=extra_scalar, vector=extra_vector, before_max=before_max),
                        lag=LAG3, steps=STEPS,
                        normed=lambda b, h: ON[:, b % 2, :, HD * h:HD * (h + 2)].rearrange("p c (h d) -> p c h d", d=HD))

    def tensor(pe, own):
        pe.wait_ge(c.loaded[n], 16)
        pe.wait_ge(c.sem("xt_ready"), 2 * k + 2)
        pe.wait_ge(fills, 2)
        for ch in range(8):
            last = nc.tensor.matmul(PS[0:1, 7, 0:128], W["bv"][:, ch:ch + 1], W["wo"][:, 128 * ch:128 * ch + 128], start=ch == 0, stop=ch == 7)
        last.then_inc(bout_psum, 1)
        pe.wait_ge(bout_ready, 1)
        for j in range(FIRST):
            run_job(pe, j)
        pe.wait_ge(free, FIRST)
        main["tensor"](pe, own)

    def scalar(act, own):
        act.wait_ge(bias_ready, 1)
        for j in range(FIRST):
            leave(act, j)
        main["scalar"](act, own)

    def vector(dve, own):
        dve.wait_ge(c.loaded[n], 16)
        nc.vector.tensor_scalar(bqs, W["bq"], HD ** -0.5, None, ALU.mult).then_inc(bias_ready, 1)
        dve.wait_ge(bout_psum, 1)
        nc.vector.tensor_tensor(bout, PS[0:1, 7, 0:128], W["bo"], ALU.add).then_inc(bout_ready, 1)
        main["vector"](dve, own)
        dve.wait_ge(free, len(jobs))

    def gpsimd(pool, own):
        pool.wait_ge(c.sem("ln_var_ready"), TILES * (k + 1))
        nc.gpsimd.memset(VB[:, :, :, :, HD:HD + 1], 1.0).then_inc(fills, 1)
        nc.gpsimd.memset(MTR, 0.0).then_inc(fills, 1)

    def sync(sp, own):
        sp.wait_ge(fills, 2)
        main["sync"](sp, own)

    return dict(tensor=tensor, scalar=scalar, vector=vector, gpsimd=gpsimd, sync=sync)


def reload(c, k, blocks, ins):
    def sync(sp, own):
        sp.wait_ge(c.sem("xt_ready"), 2 * k + 1)
        for block in blocks:
            sp.dma_start(c.weights[block], ins["w_" + block]).then_inc(c.loaded[block], 16)
    return dict(sync=sync)


def setup(c, ins):
    nc = c.nc
    ctx_psum, ctx_ready = c.sem("ctx_psum"), c.sem("ctx_ready")

    def sync(sp, own):
        sp.dma_start(c.X, ins["x"].rearrange("(t p) d -> p t d", p=128)).then_inc(c.x_loaded, 16)
        sp.dma_start(c.const_tile, ins["consts"]).then_inc(c.consts_loaded, 16)
        sp.dma_start(c.CTX, ins["ctx"].rearrange("(t p) d -> p t d", p=128)).then_inc(c.ctx_loaded, 16)
        sp.dma_start(c.small_tile, ins["small"].bitcast(BF16)).then_inc(c.small_loaded, 16)
        for block in c.stages:
            if any(block in later for later in c.reload_at.values()):
                continue
            sp.dma_start(c.weights[block], ins["w_" + block]).then_inc(c.loaded[block], 16)

    def gpsimd(pool, own):
        nc.gpsimd.memset(c.neghalf, -0.5).then_inc(c.sem("fills"), 1)
        nc.gpsimd.memset(c.ones_row, 1.0).then_inc(c.sem("fills"), 1)
        pool.wait_ge(c.sem("fills"), 2)

    def vector(dve, own):
        dve.wait_ge(c.x_loaded, 16)

    def tensor(pe, own):
        pe.wait_ge(c.consts_loaded, 16)
        pe.wait_ge(c.ctx_loaded, 16)
        pe.wait_ge(c.small_loaded, 16)
        pe.wait_ge(c.sem("fills"), 2)
        for t in range(TILES):
            nc.tensor.transpose(c.PS[:, 2 + t // 4, (t % 4) * 128:(t % 4 + 1) * 128], c.CTX[:, t, :], c.ident).then_inc(ctx_psum, 1)
        pe.wait_ge(ctx_ready, 2)

    def scalar(act, own):
        for half in range(HALVES):
            act.wait_ge(ctx_psum, 4 * half + 4)
            nc.scalar.copy(c.CTXT[:, 512 * half:512 * half + 512], c.PS[:, 2 + half, :]).then_inc(ctx_ready, 1)

    return dict(sync=sync, gpsimd=gpsimd, vector=vector, tensor=tensor, scalar=scalar)


def build(nc, ins, out, stages):
    c = Core()
    with ExitStack() as ctx:
        c.nc, c.stages = nc, stages
        lasting, passing = {}, {}
        LASTING = ("ln_var_ready", "ln_rstd_ready", "xn_ready", "xt_psum", "xt_ready", "fills", "result_ready", "stored",
                   "x_loaded", "consts_loaded", "ctx_loaded", "small_loaded")

        def sem(name):
            for group in (lasting, passing):
                if name in group:
                    return group[name]
            group = lasting if name in LASTING or name.endswith("_loaded") or name.endswith("_own") else passing
            group[name] = nc.alloc_semaphore(name=name)
            return group[name]

        stored, result_ready = sem("stored"), sem("result_ready")

        def sb(name, shape, dtype=F32):
            return ctx.enter_context(nc.sbuf_tensor(name, shape, dtype))[tuple(slice(None) for _ in shape)]

        c.sem = sem
        c.PS = ctx.enter_context(nc.psum_tensor("PS", [128, 8, 512], F32))[:, :, :]
        c.X, c.XN, c.CTX = (sb(n, [128, TILES, D]) for n in ("X", "XN", "CTX"))
        c.XT, c.CTXT = sb("XT", [128, TOKENS]), sb("CTXT", [128, TOKENS])
        c.stats, c.moments = sb("stats", [128, TILES, 6]), sb("moments", [128, TILES, 2])
        c.rstd, c.var_eps, c.neghalf = (sb(n, [128, 64]) for n in ("rstd", "var_eps", "neghalf"))
        c.ones_row = sb("ones_row", [128, 128])
        c.route_rest, c.route_max = sb("route_rest", [128, TILES, 16]), sb("route_max", [128, TILES])
        c.const_tile = sb("const_tile", [128, sum(CONST.values())])
        c.const, at = {}, 0
        for name, w in CONST.items():
            c.const[name] = c.const_tile[:, at:at + w]
            at += w
        c.ident = c.const["ident"]
        c.small_tile = sb("small_tile", [128, 512 + 2048], BF16)
        c.identb, c.mask_qk, c.mask_kq, c.ones3 = (c.small_tile[:, 128 * i:128 * i + 128] for i in range(4))
        c.sel = c.small_tile[:, 512:].rearrange("p (e f) -> p e f", e=16)
        c.x_loaded, c.consts_loaded, c.ctx_loaded, c.small_loaded = (sem(n) for n in ("x_loaded", "consts_loaded", "ctx_loaded", "small_loaded"))
        c.loaded = {b: sem(b + "_loaded") for b in stages}
        c.W, c.weights = {}, {}
        regions = ((("l0_ffn", "l0_attn", "l0_xattn", "l1_attn", "l2_attn", "l2_xattn"), ("l3_ffn",)),
                   (("l1_xattn", "l1_ffn"), ("l2_ffn", "l3_attn", "l3_xattn")))
        c.reload_at = {}
        for r, phases in enumerate(regions):
            region = sb("weights_%d" % r, [128, max(sum(columns(b) for b in p) for p in phases)])
            early = [stages.index(b) for b in phases[0] + (("l3_attn",) if r == 0 else ()) if b in stages]
            if r == 0:
                c.annex = Space(region, columns("l0_ffn"))
            for i, phase in enumerate(phases):
                at_region = 0
                for b in phase:
                    if b not in stages:
                        continue
                    if i == 1 and early:
                        c.reload_at.setdefault(max(early) + 1, []).append(b)
                    tile = region[:, at_region:at_region + columns(b)]
                    at_region += columns(b)
                    c.weights[b], c.W[b], at = tile, {}, 0
                    for name, (rows, cols) in WEIGHTS[b].items():
                        c.W[b][name] = tile[0:rows, at:at + cols]
                        at += cols
        size = SPACE
        c.space = Space(sb("space", [128, size]), size)
        c.add = lambda name: add_output(c, name)
        c.ins = ins
        orders = {e: sem(e + "_own") for e in ("tensor", "vector", "scalar", "gpsimd", "sync")}
        counts = dict.fromkeys(orders, 0)
        for first in range(0, len(stages), PHASE):
            phase = stages[first:first + PHASE]
            programs = [setup(c, ins)] if first == 0 else []
            for k, b in enumerate(phase, first):
                c.space.reset()
                c.annex.reset()
                if k in c.reload_at:
                    programs.append(reload(c, k, c.reload_at[k], ins))
                programs.append(layernorm(c, k))
                programs.append(BUILDERS[b](c, k))

            def run(engine, which):
                own = Order(engine, orders[which])
                own.n = counts[which]
                for p in programs:
                    if which in p:
                        p[which](engine, own)
                counts[which] = own.n
                return own

            last = first + PHASE >= len(stages)
            with nc.Block() as block:
                @block.tensor
                def _(pe):
                    run(pe, "tensor")

                @block.scalar
                def _(act):
                    run(act, "scalar")

                @block.gpsimd
                def _(pool):
                    run(pool, "gpsimd")

                @block.vector
                def _(dve):
                    own = run(dve, "vector")
                    if last:
                        own.settle()
                        nc.vector.tensor_copy(c.XN[:, 0:1, 0:1], c.XN[:, 0:1, 0:1]).then_inc(result_ready, 1)

                @block.sync
                def _(sp):
                    run(sp, "sync")
                    if last:
                        sp.wait_ge(result_ready, 1)
                        sp.dma_start(out.rearrange("(t p) d -> p t d", p=128), c.X).then_inc(stored, 16)
                        sp.wait_ge(stored, 16)
            if not last:
                nc.clear_and_free_semaphores(list(passing.values()))
                passing.clear()
                nc.all_engine_barrier()


BUILDERS = dict(l0_attn=l0_attn, l0_xattn=l0_xattn, l0_ffn=l0_ffn, l1_attn=l1_attn, l1_xattn=l1_xattn, l1_ffn=l1_ffn,
                l2_attn=l2_attn, l2_xattn=l2_xattn, l2_ffn=l2_ffn, l3_attn=l3_attn, l3_xattn=l3_xattn, l3_ffn=l3_ffn)
PHASE = 4
SPACE = 22200


def weights_of(inp, block):
    a = {n[len(block) + 1:]: np.asarray(v) for n, v in inp.items() if n.startswith(block + "_")}
    swap = lambda w: w.reshape(*w.shape[:-1], -1, 2)[..., ::-1].reshape(w.shape)
    col = lambda v: v.reshape(-1, 1)
    by_place = lambda w: np.moveaxis(w.reshape(-1, 8, 2, 8), 1, 3).reshape(w.shape)
    if block == "l0_attn":
        def pad(w):
            o = np.zeros((128, 8, 32), np.float32)
            o[:, :, :16] = w.transpose(1, 0, 2)
            return o.reshape(128, 256)
        return dict(wq=pad(a["W_Q"]), wqs=pad(swap(a["W_Q"])), wk=pad(a["W_K"]), wks=pad(swap(a["W_K"])),
                    wv=a["W_V"].transpose(1, 0, 2), wg=a["W_G"], wo=a["W_O"], gnw=col(a["gn_weight"]), gnb=col(a["gn_bias"]))
    if block == "l0_xattn":
        return dict(wq=by_place(a["w_q"]), wk=a["w_kv"][:, :8], wv=a["w_kv"][:, 8:], wo=a["w_concat"])
    if block in ("l2_attn", "l2_xattn"):
        return dict(wq=by_place(a["Wq"]), wk=by_place(a["Wk"]), wv=a["Wv"], wo=a["Wo"], bq=by_place(a["bq"]),
                    bk=by_place(a["bk"]), bv=a["bv"], bo=a["bo"])
    if block == "l0_ffn":
        return dict(router=a["router_w"].T, gate_up=a["gate_up_proj"].transpose(1, 0, 2), down=a["down_proj"].transpose(1, 0, 2),
                    s_gate=a["shared_gate_w"].T, s_up=a["shared_up_w"].T,
                    s_down=a["shared_down_w"].T.reshape(4, 128, 128).transpose(1, 0, 2))
    if block == "l1_attn":
        return dict(q=col(a["q"]), k=col(a["k"]), log_decay=col(np.repeat(a["log_decay"], 8)), norm=col(a["norm_weight"]),
                    wo=a["o_w"].T, headsum=np.kron(np.eye(16), np.ones((8, 8))).astype(np.float32))
    if block == "l1_ffn":
        gu, gb = a["gate_up_proj"].transpose(1, 0, 2), a["gate_up_proj_bias"]
        return dict(gate=gu[:, :, ::2], up=gu[:, :, 1::2], gate_b=gb[:, ::2].T, up_b=gb[:, 1::2].T,
                    down=a["down_proj"].transpose(1, 0, 2), down_b=a["down_proj_bias"],
                    route_w=a["routing_weights"].reshape(2, 128, 8).transpose(1, 0, 2))
    if block == "l3_ffn":
        both = lambda n: np.concatenate([a["shared_" + n][None], a["routed_" + n]])
        return dict(router=a["router_w"].T, gate=both("gate").transpose(2, 0, 1), up=both("up").transpose(2, 0, 1),
                    down=both("down").reshape(8, 128, 4, 128).transpose(3, 0, 2, 1))
    if block == "l2_ffn":
        rep = lambda v: np.broadcast_to(v, (128, v.shape[0]))
        return dict(w1=a["w1"].T, b1=rep(a["b1"]), w2=a["w2"].T.reshape(4, 128, 128).transpose(1, 0, 2), b2=rep(a["b2"]),
                    ln1w=rep(a["ln1_w"]), ln1b=rep(a["ln1_b"]), ln2w=rep(a["ln2_w"]), ln2b=rep(a["ln2_b"]))
    if block == "l3_xattn":
        return dict(wq=a["Wq"].T, wk=a["Wk"].T, wv=a["Wv"].T, wo=a["Wo"].T, bq=a["bq"], bk=a["bk"], bv=a["bv"], bo=a["bo"],
                    ln_g=col(a["ln_g"]), ln_b=col(a["ln_b"]))
    if block == "l1_xattn":
        up = lambda w: w.reshape(-1, 16, 64).transpose(2, 1, 0)
        return dict(kv_comp=a["w_kv_comp"], q_down=a["w_q_down"], q_upT=up(a["w_q_up"]), q_rope=a["w_q_rope"],
                    k_upT=up(a["w_k_up"]), k_rope=a["w_k_rope"], v_upT=up(a["w_v_up"]), out=a["w_out"].reshape(16, 64, 128).transpose(1, 0, 2))
    if block == "l3_attn":
        return dict(wq=a["Wq"], wk=a["Wk"], wv=a["Wv"], wo=a["Wo"].reshape(8, 128, 128).transpose(1, 0, 2),
                    bq=a["bq"].reshape(8, 128).T, bk=a["bk"].reshape(8, 128).T, bv=a["bv"].reshape(8, 128).T, bo=a["bo"])
    raise KeyError(block)


def arrays_of(inputs, stages):
    low = {n[0].lower() + n[1:] if n.startswith("L") else n: v for n, v in inputs.items()}
    arrays = {"x": np.ascontiguousarray(np.asarray(inputs["x"]).reshape(TOKENS, D)),
              "ctx": np.ascontiguousarray(np.asarray(inputs["ctx_1024"]).reshape(TOKENS, D)),
              "seg": np.ascontiguousarray(np.asarray(inputs["itok_BxS_0_511"]).reshape(1, TOKENS)),
              "seg_rows": np.ascontiguousarray(np.asarray(inputs["itok_BxS_0_511"]).reshape(TILES, 128).T),
              "route": np.ascontiguousarray(np.asarray(inputs["L1_ffn_router_indices"]).reshape(2, 128, 2).transpose(1, 0, 2).reshape(128, 4)),
              "consts": constants(), "small": small_constants()}
    arrays["stack_q"], arrays["stack_k"] = stack_constants()
    for b in stages:
        arrays["w_" + b] = pack(b, weights_of(low, b))
    return arrays


def program(nc, arrays, stages):
    ins = {n: nc.dram_tensor("in_" + n, a.shape, mybir.dt.from_np(a.dtype), kind="ExternalInput").ap() for n, a in arrays.items()}
    out = nc.dram_tensor("out_x", [TOKENS, D], F32, kind="ExternalOutput").ap()
    build(nc, ins, out, stages)


def kernel(**inputs):
    import concourse.bacc as _bacc
    from concourse.bass_utils import run_bass_kernel_spmd as _run
    nc = _bacc.Bacc("TRN2", target_bir_lowering=False, num_devices=1)
    arrays = arrays_of(inputs, BLOCKS)
    program(nc, arrays, BLOCKS)
    r = _run(nc, [{"in_" + n: a for n, a in arrays.items()}], core_ids=[0])
    return r.results[0]["out_x"].reshape(B, L, D)
```
